# Optimizing a Trainium2 kernel written in Bass

```python
import numpy as np
import jax
import jax.numpy as jnp

def _softmax(x, axis=-1):
    return jax.nn.softmax(x, axis=axis)

def _gelu(x):
    return jax.nn.gelu(x, approximate=True)

def _silu(x):
    return jax.nn.silu(x)

def _sigmoid(x):
    return jax.nn.sigmoid(x)

def _layernorm(x, axis=-1, eps=1e-05):
    m = jnp.mean(x, axis=axis, keepdims=True)
    v = jnp.var(x, axis=axis, keepdims=True)
    return (x - m) / jnp.sqrt(v + eps)

def _scatter_add(tgt, idx, src, axis=0):
    return tgt.at[idx].add(src)

def _segment_sum(src, seg, n):
    return jax.ops.segment_sum(src, seg, n)
kernel_name = 'mk_cond_seq_d2_seqx_r4_787b85'

def setup_inputs(seed: int=0):
    np.random.seed(seed)
    _w = jnp.asarray

    def _rec_inputs():
        import jax
        import jax.numpy as jnp
        _rk = jax.random.key(seed)
        x = 1.648e-05 + 1 * jax.random.normal(jax.random.fold_in(_rk, 1), (2, 1024, 288), jnp.float32)
        _lenS = 1024 - jax.random.randint(jax.random.fold_in(_rk, 7), (2,), 0, max(1, 1024 // 4) + 1, jnp.int32)
        _lenS2 = 1024 - jax.random.randint(jax.random.fold_in(_rk, 8), (2,), 0, max(1, 1024 // 4) + 1, jnp.int32)
        cond_1152 = 0.00914911 + 1.00357 * jax.random.normal(jax.random.fold_in(_rk, 11), (2, 288), jnp.float32)
        return (x, cond_1152)
    x, cond_1152 = _rec_inputs()

    def _L0_cond_setup():
        import jax, jax.numpy as jnp
        import numpy as np
        B, L, C = (8, 256, 288)
        H = 16
        D = C // H
        FF = int(C * 4.0)
        EPS = 1e-06

        def _layernorm(x):
            mu = jnp.mean(x, axis=-1, keepdims=True)
            var = jnp.mean(jnp.square(x - mu), axis=-1, keepdims=True)
            return (x - mu) * jax.lax.rsqrt(var + EPS)

        def _modulate(x, shift, scale):
            return x * (1.0 + scale) + shift

        def _attention(h, W_qkv, b_qkv, W_proj, b_proj):
            b, l, c = h.shape
            qkv = h @ W_qkv + b_qkv
            qkv = qkv.reshape(b, l, 3, H, D)
            q, k, v = (qkv[:, :, 0], qkv[:, :, 1], qkv[:, :, 2])
            scale = D ** (-0.5)
            scores = jnp.einsum('blhd,bmhd->bhlm', q * scale, k)
            attn = jax.nn.softmax(scores, axis=-1)
            o = jnp.einsum('bhlm,bmhd->blhd', attn, v).reshape(b, l, c)
            return o @ W_proj + b_proj
        key = jax.random.key(seed)
        ks = jax.random.split(key, 12)
        s = 0.02
        return {'x': jax.random.normal(ks[0], (B, L, C), jnp.float32), 'c': jax.random.normal(ks[1], (B, 1, C), jnp.float32), 'W_qkv': jax.random.normal(ks[2], (C, 3 * C), jnp.float32) * s, 'b_qkv': jnp.zeros((3 * C,), jnp.float32), 'W_proj': jax.random.normal(ks[3], (C, C), jnp.float32) * s, 'b_proj': jnp.zeros((C,), jnp.float32), 'W_fc1': jax.random.normal(ks[4], (C, FF), jnp.float32) * s, 'b_fc1': jnp.zeros((FF,), jnp.float32), 'W_fc2': jax.random.normal(ks[5], (FF, C), jnp.float32) * s, 'b_fc2': jnp.zeros((C,), jnp.float32), 'W_ada': jax.random.normal(ks[6], (C, 6 * C), jnp.float32) * s, 'b_ada': jnp.zeros((6 * C,), jnp.float32)}
    _L0_cond_all = _L0_cond_setup()
    _L0_cond_in = {k: v for k, v in _L0_cond_all.items() if k in ('W_qkv', 'b_qkv', 'W_proj', 'b_proj', 'W_fc1', 'b_fc1', 'W_fc2', 'b_fc2', 'W_ada', 'b_ada')}
    del _L0_cond_all

    def _L1_cond_setup():
        import jax, jax.numpy as jnp
        import numpy as np
        NUM_HEADS = 16
        NUM_EXPERTS = 4
        TOP_K = 2
        LN_EPS = 1e-06

        def _ln(h):
            mu = jnp.mean(h, axis=-1, keepdims=True)
            var = jnp.var(h, axis=-1, keepdims=True)
            return (h - mu) * jax.lax.rsqrt(var + LN_EPS)

        def _modulate(h, shift, scale):
            return h * (1.0 + scale[:, None, :]) + shift[:, None, :]
        key = jax.random.key(seed)
        ks = jax.random.split(key, 12)
        B, N, C = (8, 256, 288)
        H = 4 * C
        E = NUM_EXPERTS
        s = 0.02
        return {'x': jax.random.normal(ks[0], (B, N, C), jnp.float32), 'c': jax.random.normal(ks[1], (B, C), jnp.float32), 'w_adaln': jax.random.normal(ks[2], (C, 6 * C), jnp.float32) * s, 'b_adaln': jnp.zeros((6 * C,), jnp.float32), 'w_qkv': jax.random.normal(ks[3], (C, 3 * C), jnp.float32) * s, 'b_qkv': jnp.zeros((3 * C,), jnp.float32), 'w_proj': jax.random.normal(ks[4], (C, C), jnp.float32) * s, 'b_proj': jnp.zeros((C,), jnp.float32), 'w_gate': jax.random.normal(ks[5], (C, E), jnp.float32) * s, 'w1': jax.random.normal(ks[6], (E, C, H), jnp.float32) * s, 'b1': jnp.zeros((E, H), jnp.float32), 'w2': jax.random.normal(ks[7], (E, H, C), jnp.float32) * s, 'b2': jnp.zeros((E, C), jnp.float32)}
    _L1_cond_all = _L1_cond_setup()
    _L1_cond_in = {k: v for k, v in _L1_cond_all.items() if k in ('w_adaln', 'b_adaln', 'w_qkv', 'b_qkv', 'w_proj', 'b_proj', 'w_gate', 'w1', 'b1', 'w2', 'b2')}
    del _L1_cond_all
    return {'x': x, 'cond_1152': cond_1152, 'L0_cond_W_qkv': _L0_cond_in['W_qkv'], 'L0_cond_b_qkv': _L0_cond_in['b_qkv'], 'L0_cond_W_proj': _L0_cond_in['W_proj'], 'L0_cond_b_proj': _L0_cond_in['b_proj'], 'L0_cond_W_fc1': _L0_cond_in['W_fc1'], 'L0_cond_b_fc1': _L0_cond_in['b_fc1'], 'L0_cond_W_fc2': _L0_cond_in['W_fc2'], 'L0_cond_b_fc2': _L0_cond_in['b_fc2'], 'L0_cond_W_ada': _L0_cond_in['W_ada'], 'L0_cond_b_ada': _L0_cond_in['b_ada'], 'L1_cond_w_adaln': _L1_cond_in['w_adaln'], 'L1_cond_b_adaln': _L1_cond_in['b_adaln'], 'L1_cond_w_qkv': _L1_cond_in['w_qkv'], 'L1_cond_b_qkv': _L1_cond_in['b_qkv'], 'L1_cond_w_proj': _L1_cond_in['w_proj'], 'L1_cond_b_proj': _L1_cond_in['b_proj'], 'L1_cond_w_gate': _L1_cond_in['w_gate'], 'L1_cond_w1': _L1_cond_in['w1'], 'L1_cond_b1': _L1_cond_in['b1'], 'L1_cond_w2': _L1_cond_in['w2'], 'L1_cond_b2': _L1_cond_in['b2']}

def reference(x, cond_1152, L0_cond_W_qkv, L0_cond_b_qkv, L0_cond_W_proj, L0_cond_b_proj, L0_cond_W_fc1, L0_cond_b_fc1, L0_cond_W_fc2, L0_cond_b_fc2, L0_cond_W_ada, L0_cond_b_ada, L1_cond_w_adaln, L1_cond_b_adaln, L1_cond_w_qkv, L1_cond_b_qkv, L1_cond_w_proj, L1_cond_b_proj, L1_cond_w_gate, L1_cond_w1, L1_cond_b1, L1_cond_w2, L1_cond_b2):
    import jax
    import jax.numpy as jnp

    def _L0_cond_ref(x, c, W_qkv, b_qkv, W_proj, b_proj, W_fc1, b_fc1, W_fc2, b_fc2, W_ada, b_ada):
        import jax, jax.numpy as jnp
        import numpy as np
        B, L, C = (8, 256, 288)
        H = 16
        D = C // H
        FF = int(C * 4.0)
        EPS = 1e-06

        def _layernorm(x):
            mu = jnp.mean(x, axis=-1, keepdims=True)
            var = jnp.mean(jnp.square(x - mu), axis=-1, keepdims=True)
            return (x - mu) * jax.lax.rsqrt(var + EPS)

        def _modulate(x, shift, scale):
            return x * (1.0 + scale) + shift

        def _attention(h, W_qkv, b_qkv, W_proj, b_proj):
            b, l, c = h.shape
            qkv = h @ W_qkv + b_qkv
            qkv = qkv.reshape(b, l, 3, H, D)
            q, k, v = (qkv[:, :, 0], qkv[:, :, 1], qkv[:, :, 2])
            scale = D ** (-0.5)
            scores = jnp.einsum('blhd,bmhd->bhlm', q * scale, k)
            attn = jax.nn.softmax(scores, axis=-1)
            o = jnp.einsum('bhlm,bmhd->blhd', attn, v).reshape(b, l, c)
            return o @ W_proj + b_proj
        ada = jax.nn.silu(c) @ W_ada + b_ada
        shift_msa, scale_msa, gate_msa, shift_mlp, scale_mlp, gate_mlp = jnp.split(ada, 6, axis=-1)
        h = _modulate(_layernorm(x), shift_msa, scale_msa)
        x = x + gate_msa * _attention(h, W_qkv, b_qkv, W_proj, b_proj)
        h = _modulate(_layernorm(x), shift_mlp, scale_mlp)
        mlp = jax.nn.gelu(h @ W_fc1 + b_fc1, approximate=True) @ W_fc2 + b_fc2
        x = x + gate_mlp * mlp
        return x

    def _L1_cond_ref(x, c, w_adaln, b_adaln, w_qkv, b_qkv, w_proj, b_proj, w_gate, w1, b1, w2, b2):
        import jax, jax.numpy as jnp
        import numpy as np
        NUM_HEADS = 16
        NUM_EXPERTS = 4
        TOP_K = 2
        LN_EPS = 1e-06

        def _ln(h):
            mu = jnp.mean(h, axis=-1, keepdims=True)
            var = jnp.var(h, axis=-1, keepdims=True)
            return (h - mu) * jax.lax.rsqrt(var + LN_EPS)

        def _modulate(h, shift, scale):
            return h * (1.0 + scale[:, None, :]) + shift[:, None, :]
        B, N, C = x.shape
        nh = NUM_HEADS
        hd = C // nh
        mod = jax.nn.silu(c) @ w_adaln + b_adaln
        sh_msa, sc_msa, g_msa, sh_mlp, sc_mlp, g_mlp = jnp.split(mod, 6, axis=-1)
        h = _modulate(_ln(x), sh_msa, sc_msa)
        qkv = (h @ w_qkv + b_qkv).reshape(B, N, 3, nh, hd).transpose(2, 0, 3, 1, 4)
        q, k, v = (qkv[0], qkv[1], qkv[2])
        attn = jax.nn.softmax(jnp.einsum('bhqd,bhkd->bhqk', q, k) * hd ** (-0.5), axis=-1)
        o = jnp.einsum('bhqk,bhkd->bhqd', attn, v).transpose(0, 2, 1, 3).reshape(B, N, C)
        o = o @ w_proj + b_proj
        x = x + g_msa[:, None, :] * o
        xn = _modulate(_ln(x), sh_mlp, sc_mlp)
        xf = xn.reshape(-1, C)
        gate_logits = xf @ w_gate
        topk_logits, topk_idx = jax.lax.top_k(gate_logits, TOP_K)
        gates = jax.nn.softmax(topk_logits, axis=-1)
        cw = jnp.sum(jax.nn.one_hot(topk_idx, NUM_EXPERTS, dtype=xf.dtype) * gates[..., None], axis=1)
        hmid = jax.nn.gelu(jnp.einsum('tc,ech->eth', xf, w1) + b1[:, None, :], approximate=True)
        eo = jnp.einsum('eth,ehc->etc', hmid, w2) + b2[:, None, :]
        moe = jnp.einsum('te,etc->tc', cw, eo).reshape(B, N, C)
        return x + g_mlp[:, None, :] * moe
    x = _L0_cond_ref(x, cond_1152[:, None, :], L0_cond_W_qkv, L0_cond_b_qkv, L0_cond_W_proj, L0_cond_b_proj, L0_cond_W_fc1, L0_cond_b_fc1, L0_cond_W_fc2, L0_cond_b_fc2, L0_cond_W_ada, L0_cond_b_ada)
    x = _L1_cond_ref(x, cond_1152, L1_cond_w_adaln, L1_cond_b_adaln, L1_cond_w_qkv, L1_cond_b_qkv, L1_cond_w_proj, L1_cond_b_proj, L1_cond_w_gate, L1_cond_w1, L1_cond_b1, L1_cond_w2, L1_cond_b2)
    return x

_drawn_inputs = setup_inputs


def setup_inputs(seed=0):
    import zlib

    import numpy as np

    out = dict(_drawn_inputs(seed))
    spreads = {'L0_cond_b_qkv': (0.0, 0.8),
     'L0_cond_b_proj': (0.0, 0.341),
     'L0_cond_b_fc1': (0.0, 0.8),
     'L0_cond_b_fc2': (0.0, 0.362),
     'L0_cond_b_ada': (0.0, 0.387),
     'L1_cond_b_adaln': (0.0, 0.447),
     'L1_cond_b_qkv': (0.0, 0.8),
     'L1_cond_b_proj': (0.0, 0.379),
     'L1_cond_b1': (0.0, 0.8),
     'L1_cond_b2': (0.0, 0.512)}
    factors = {'L0_cond_W_qkv': 8.0,
     'L0_cond_W_proj': 5.309,
     'L1_cond_w_qkv': 8.0,
     'L1_cond_w_proj': 5.557,
     'L1_cond_w_gate': 2.901,
     'L1_cond_w1': 2.831}
    for name, (base, spread) in spreads.items():
        noise = np.random.default_rng([zlib.crc32(name.encode()), seed]).standard_normal(out[name].shape)
        drawn = base * np.exp(spread * noise) if base else spread * noise
        out[name] = jnp.asarray(drawn.astype(out[name].dtype))
    for name, factor in factors.items():
        out[name] = (out[name] * factor).astype(out[name].dtype)
    return out
```

```python
from contextlib import ExitStack

import concourse.bass as bass
from concourse import mybir

ACT = mybir.ActivationFunctionType
ALU = mybir.AluOpType
AX_X = mybir.AxisListType.X
F32 = mybir.dt.float32
F32R = mybir.dt.float32r
BF16 = mybir.dt.bfloat16
ds = bass.ds

P = 128
B, SEQ, C, H = 2, 1024, 288, 16
D = C // H
FF = 4 * C
E = 4
TOKENS = B * SEQ
TILES = TOKENS // P
KC, CK = 3, C // 3
NF = FF // P
BLK = 512
TPB = BLK // P
NBLK = TOKENS // BLK
HALVES = SEQ // BLK
EPS = 1e-6
SCALE = float(D) ** -0.5
HG = 4
GPB = H // HG
GROUPS = B * GPB
KT = SEQ // P
PARTS = ((0, 0), (1, 0), (0, 1))
Q_TERMS, K_TERMS = (0, 0, 0, 1, 1, 2), (0, 1, 2, 0, 1, 0)
ROWS = len(Q_TERMS) * D
QK_HEADS = 2 * H
CHUNK_HEADS = P // D
QK_CHUNKS = -(-QK_HEADS // CHUNK_HEADS)


def chunk_rows(c):
    return min(CHUNK_HEADS, QK_HEADS - CHUNK_HEADS * c) * D


def chunk_pieces(c):
    heads = range(CHUNK_HEADS * c, min(CHUNK_HEADS * (c + 1), QK_HEADS))
    out = []
    for n in sorted({h // HG for h in heads}):
        own = [h for h in heads if h // HG == n]
        out.append(((own[0] - heads[0]) * D, len(own) * D, n // GPB, n % GPB, own[0] % HG * D))
    return out


def row(ap, n):
    return ap.rearrange("(o c) -> o c", o=1).broadcast_to([n, ap.shape[0]])


def scopes(nc, ctx, stage):
    def sb(name, shape, dt):
        return ctx.enter_context(nc.sbuf_tensor(f"{stage}_{name}", shape, dt))

    def banks(name, n, width=1):
        shape = [P, 512] if width == 1 else [P, width, 512]
        return [ctx.enter_context(nc.psum_tensor(f"{stage}_{name}{i}", shape, F32)) for i in range(n)]

    sems = []

    @ctx.callback
    def _():
        nc.clear_and_free_semaphores(sems)
        nc.all_engine_barrier()

    def sem(name):
        sems.append(nc.alloc_semaphore(name=f"{stage}_{name}"))
        return sems[-1]

    return sb, banks, sem


def modulation(nc, T, x, cond, layers):
    with ExitStack() as ctx:
        sb, banks, sem = scopes(nc, ctx, "ada")
        NA = 4
        AW = 6 * C // NA
        cT = sb("cT", [CK, KC, B], F32)
        sc = sb("sc", [CK, KC, B], F32)
        ones = sb("ones", [CK, P], F32)
        screp = sb("screp", [CK, KC, B, P], F32)
        w = [sb(f"w_ada{l}", [CK, KC, 6 * C], F32) for l in range(2)]
        brow = [sb(f"b_ada_rows{l}", [B, 6 * C], F32) for l in range(2)]
        bgate = [sb(f"b_gate{l}", [P, 2, C], F32) for l in range(2)]
        arow = [sb(f"ada_rows{l}", [B, 6 * C], F32) for l in range(2)]
        ps = banks("ada", NA)
        psT = banks("adaT", 1)[0]
        psG = banks("gateP", 2)

        small_in = sem("small_in")
        w_in = [sem(f"w_in{l}") for l in range(2)]
        x_in = sem("x_in")
        ident0 = sem("ident0")
        ident_ready = sem("ident_ready")
        ones_ready = sem("ones_ready")
        silu_ready = sem("silu_ready")
        rep_ready = sem("rep_ready")
        rows_ready = sem("rows_ready")
        rows_out = sem("rows_out")
        cols_ready = sem("cols_ready")
        cols_out = sem("cols_out")
        gate_ready = sem("gate_ready")
        gate_out = sem("gate_out")

        block = ctx.enter_context(nc.Block())

        @block.sync
        def _(sp):
            for b in range(B):
                for j in range(KC):
                    sp.dma_start(cT[:, j, b:b + 1], cond[b, j * CK:(j + 1) * CK].rearrange("(p o) -> p o", o=1)
                                 ).then_inc(small_in, 16)
            for l in range(2):
                sp.dma_start(w[l][:], layers[l].w_ada.rearrange("(k p) n -> p k n", p=CK)).then_inc(w_in[l], 16)
                sp.dma_start(brow[l][:], row(layers[l].b_ada, B)).then_inc(small_in, 16)
                for n, part in enumerate((2, 5)):
                    sp.dma_start(bgate[l][:, n, :], row(layers[l].b_ada[part * C:(part + 1) * C], P)
                                 ).then_inc(small_in, 16)
            sp.dma_start(T.X[:], x.rearrange("b (t p) c -> p (b t) c", p=P)).then_inc(x_in, 16)
            sp.wait_ge(x_in, 16)

        @block.gpsimd
        def _(pool):
            nc.gpsimd.memset(T.ident[:], 0.0).then_inc(ident0, 1)
            pool.wait_ge(ident0, 1)
            nc.gpsimd.affine_select(out=T.ident[:], in_=T.ident[:], compare_op=ALU.not_equal, fill=1.0, base=0,
                                    pattern=[[-1, P]], channel_multiplier=1).then_inc(ident_ready, 1)

        @block.scalar
        def _(act):
            act.wait_ge(small_in, 16 * (B * KC + 6))
            nc.scalar.activation(sc[:], cT[:], ACT.Silu).then_inc(silu_ready, 1)

        @block.vector
        def _(dve):
            nc.vector.memset(ones[:], 1.0).then_inc(ones_ready, 1)
            dve.wait_ge(ones_ready, 1)
            dve.wait_ge(silu_ready, 1)
            for j in range(KC):
                for b in range(B):
                    last = nc.vector.tensor_scalar(screp[:, j, b, :], ones[:], sc[:, j, b:b + 1], None, ALU.mult)
            last.then_inc(rep_ready, 1)
            dve.wait_ge(small_in, 16 * (B * KC + 6))
            for l in range(2):
                for n in range(NA):
                    dve.wait_ge(rows_ready, NA * l + n + 1)
                    nc.vector.tensor_tensor(arow[l][:, n * AW:(n + 1) * AW], ps[n][0:B, 0:AW],
                                            brow[l][:, n * AW:(n + 1) * AW], ALU.add).then_inc(rows_out, 1)
                dve.wait_ge(cols_ready, l + 1)
                for n in range(4):
                    last = nc.vector.tensor_scalar(T.mod[l][:, n].rearrange("p j b -> p (j b)"),
                                                   psT[0:CK, n * KC * B:(n + 1) * KC * B], float(n % 2), None, ALU.add)
                last.then_inc(cols_out, 1)
                for g in range(2):
                    for b in range(B):
                        n = 4 * l + 2 * g + b
                        dve.wait_ge(gate_ready, n + 1)
                        nc.vector.tensor_tensor(T.gate[l][:, g, b, :], psG[n % 2][:, 0:C], bgate[l][:, g, :],
                                                ALU.add).then_inc(gate_out, 1)

        @block.tensor
        def _(pe):
            pe.wait_ge(silu_ready, 1)
            pe.wait_ge(ident_ready, 1)
            pe.wait_ge(rep_ready, 1)
            for l in range(2):
                pe.wait_ge(w_in[l], 16)
                for n in range(NA):
                    if l:
                        pe.wait_ge(rows_out, n + 1)
                    for j in range(KC):
                        last = nc.tensor.matmul(ps[n][0:B, 0:AW], sc[:, j, :], w[l][:, j, n * AW:(n + 1) * AW],
                                                start=(j == 0), stop=(j == KC - 1))
                    last.then_inc(rows_ready, 1)
                if l:
                    pe.wait_ge(cols_out, 1)
                pe.wait_ge(rows_out, NA * (l + 1))
                for n, part in enumerate((0, 1, 3, 4)):
                    for j in range(KC):
                        at = (n * KC + j) * B
                        c0 = part * C + j * CK
                        last = nc.tensor.transpose(psT[0:CK, at:at + B], arow[l][:, c0:c0 + CK], T.ident[0:B, 0:B])
                last.then_inc(cols_ready, 1)
                for g, part in enumerate((2, 5)):
                    for b in range(B):
                        n = 4 * l + 2 * g + b
                        if n >= 2:
                            pe.wait_ge(gate_out, n - 1)
                        for j in range(KC):
                            last = nc.tensor.matmul(psG[n % 2][:, 0:C], screp[:, j, b, :],
                                                    w[l][:, j, part * C:(part + 1) * C],
                                                    start=(j == 0), stop=(j == KC - 1))
                        last.then_inc(gate_ready, 1)


def wait_alone(eng, sem, value, passed):
    eng.wait_ge(sem, value)
    eng.sem_inc(passed, 1)


class Norm:

    def __init__(self, sb, sem):
        self.stats = sb("bn_stats", [P, TPB, 6], F32)
        self.mv = sb("mean_var", [P, TPB, 2], F32)
        self.veps = sb("var_eps", [P, TPB], F32)
        self.std = sb("std", [P, TPB], F32)
        self.rstd = sb("rstd", [P, TPB], F32)
        self.xn = sb("x_normed", [P, TPB, C], F32)
        self.h = sb("h_mod", [CK, KC, BLK], F32)
        self.steps = sem("norm_steps")
        self.passed = sem("waits_passed")
        self.var_ready = sem("var_ready")
        self.std_ready = sem("std_ready")
        self.xn_ready = sem("xn_ready")
        self.xt_ready = sem("xt_ready")
        self.h_ready = sem("h_ready")
        self.hi_ready = sem("hi_ready")
        self.parts_ready = sem("parts_ready")


def norm_tiles(nc, dve, N, X, tile0, i):
    for t in range(TPB):
        last = nc.vector.bn_stats(N.stats[:, t, :], X[:, ds(tile0 + t, 1), :].rearrange("p o c -> p (o c)"))
    last.then_inc(N.steps, 1)
    wait_alone(dve, N.steps, i * 3 + 1, N.passed)
    for t in range(TPB):
        last = nc.vector.bn_aggr(N.mv[:, t, :], N.stats[:, t, :])
    last.then_inc(N.steps, 1)
    dve.wait_ge(N.steps, i * 3 + 2)
    nc.vector.tensor_scalar(N.veps[:], N.mv[:, :, 1], EPS, None, ALU.add).then_inc(N.var_ready, 1)
    dve.wait_ge(N.std_ready, i + 1)
    nc.vector.reciprocal(N.rstd[:], N.std[:]).then_inc(N.steps, 1)
    dve.wait_ge(N.steps, i * 3 + 3)
    for t in range(TPB):
        last = nc.vector.tensor_scalar(N.xn[:, t, :], X[:, ds(tile0 + t, 1), :].rearrange("p o c -> p (o c)"),
                                       N.mv[:, t, 0:1], N.rstd[:, t:t + 1], ALU.subtract, ALU.mult)
    last.then_inc(N.xn_ready, 1)


def norm_transposes(nc, pe, N, T, psT, i):
    pe.wait_ge(N.xn_ready, i + 1)
    for j in range(KC):
        for t in range(TPB):
            last = nc.tensor.transpose(psT[j][0:CK, t * P:(t + 1) * P], N.xn[:, t, j * CK:(j + 1) * CK], T.ident[:])
        last.then_inc(N.xt_ready, 1)


def norm_modulate(nc, act, N, mod, which, psT, b, i):
    act.wait_ge(N.var_ready, i + 1)
    nc.scalar.activation(N.std[:], N.veps[:], ACT.Sqrt).then_inc(N.std_ready, 1)
    for j in range(KC):
        act.wait_ge(N.xt_ready, i * KC + j + 1)
        nc.scalar.activation(N.h[:, j, :], psT[j][0:CK, :], ACT.Identity, scale=mod[:, which + 1, j, ds(b, 1)],
                             bias=mod[:, which, j, ds(b, 1)]).then_inc(N.h_ready, 1)


def norm_split(nc, dve, N, hi, lo, i):
    for j in range(KC):
        dve.wait_ge(N.h_ready, i * KC + j + 1)
        nc.vector.tensor_copy(hi(j), N.h[:, j, :]).then_inc(N.hi_ready, 1)
    for j in range(KC):
        dve.wait_ge(N.hi_ready, i * KC + j + 1)
        last = nc.vector.tensor_tensor(lo(j), N.h[:, j, :], hi(j).bitcast(F32), ALU.subtract)
    last.then_inc(N.parts_ready, 1)


def qkv_stage(nc, T, l, W):
    with ExitStack() as ctx:
        sb, banks, sem = scopes(nc, ctx, f"qkv{l}")
        wst = sb("wqkv_f32", [CK, KC, 3 * C], F32)
        w = sb("wqkv_parts", [CK, 2, KC, 3 * C], F32R)
        bqk = sb("b_qk", [CHUNK_HEADS * D, QK_CHUNKS], F32)
        bv = sb("b_v", [P, C], F32)
        N = Norm(sb, sem)
        hT = sb("hT_parts", [CK, 2, KC, BLK], F32R)
        thirds = [sb(f"thirds{c}", [CHUNK_HEADS * D, 3, BLK], BF16) for c in range(QK_CHUNKS)]
        rest = [sb(f"rest{c}", [CHUNK_HEADS * D, BLK], F32) for c in range(QK_CHUNKS)]
        psT = banks("xT", KC)
        psQ = banks("qk", 2)
        psV = banks("v", 2)

        w_in = sem("w_in")
        b_in = sem("b_in")
        whi_ready = sem("whi_ready")
        w_ready = sem("w_ready")
        v_filled = sem("v_filled")
        mm_done = sem("mm_done")
        qk_ready = sem("qk_ready")
        v_ready = sem("v_ready")
        v_out = sem("v_out")
        first_ready = sem("first_ready")
        rest_ready = sem("rest_ready")
        second_ready = sem("second_ready")
        thirds_ready = sem("thirds_ready")
        stored = [sem(f"stored{c}") for c in range(QK_CHUNKS)]
        pieces = [len(chunk_pieces(c)) for c in range(QK_CHUNKS)]

        block = ctx.enter_context(nc.Block())

        @block.sync
        def _(sp):
            sp.dma_start(wst[:], W.w_qkv.rearrange("(k p) n -> p k n", p=CK)).then_inc(w_in, 16)
            for c in range(QK_CHUNKS):
                r = chunk_rows(c)
                c0 = c * CHUNK_HEADS * D
                sp.dma_start(bqk[0:r, c:c + 1], W.b_qkv[c0:c0 + r].rearrange("(p o) -> p o", o=1)).then_inc(b_in, 16)
            sp.dma_start(bv[:], row(W.b_qkv[2 * C:3 * C], P)).then_inc(b_in, 16)
            with sp.Fori(0, B) as b:
                with sp.Fori(0, HALVES) as half:
                    i = b * HALVES + half
                    for c in range(QK_CHUNKS):
                        sp.wait_ge(thirds_ready, i * QK_CHUNKS + c + 1)
                        for r0, r, qk, hg, off in chunk_pieces(c):
                            dst = T.qk_scr[ds(b * GPB + hg, 1), qk, :, off:off + r, ds(half * BLK, BLK)]
                            sp.dma_start(dst.rearrange("o t r n -> r (o t) n"), thirds[c][r0:r0 + r, :, :]
                                         ).then_inc(stored[c], 16)
            for c in range(QK_CHUNKS):
                sp.wait_ge(stored[c], 16 * pieces[c] * (NBLK + 1))

        @block.gpsimd
        def _(pool):
            v = T.V[:].rearrange("p g k (j d) -> p (g k j) d", j=HG)
            nc.gpsimd.memset(v[:, :, D:D + 1], 1.0).then_inc(v_filled, 1)
            nc.gpsimd.memset(v[:, :, D + 1:32], 0.0).then_inc(v_filled, 1)
            pool.wait_ge(v_filled, 2)

        @block.scalar
        def _(act):
            act.wait_ge(b_in, 16 * (QK_CHUNKS + 1))
            for c in range(QK_CHUNKS):
                act.sem_inc(stored[c], 16 * pieces[c])
            with act.Fori(0, B) as b:
                with act.Fori(0, HALVES) as half:
                    i = b * HALVES + half
                    norm_modulate(nc, act, N, T.mod[l], 0, psT, b, i)

                    def second(c):
                        r = chunk_rows(c)
                        act.wait_ge(rest_ready, i * QK_CHUNKS + c + 1)
                        nc.scalar.activation(thirds[c][0:r, 1, :], rest[c][0:r, :], ACT.Identity
                                             ).then_inc(second_ready, 1)

                    for c in range(QK_CHUNKS):
                        r = chunk_rows(c)
                        act.wait_ge(qk_ready, i * QK_CHUNKS + c + 1)
                        act.wait_ge(stored[c], (i + 1) * (16 * pieces[c]))
                        nc.scalar.activation(thirds[c][0:r, 0, :], psQ[c % 2][0:r, :], ACT.Identity,
                                             bias=bqk[0:r, c:c + 1]).then_inc(first_ready, 1)
                        if c:
                            second(c - 1)
                    second(QK_CHUNKS - 1)

        @block.vector
        def _(dve):
            dve.sem_inc(v_out, 2)
            dve.wait_ge(w_in, 16)
            nc.vector.tensor_copy(w[:, 0], wst[:]).then_inc(whi_ready, 1)
            dve.wait_ge(whi_ready, 1)
            nc.vector.tensor_tensor(w[:, 1], wst[:], w[:, 0].bitcast(F32), ALU.subtract).then_inc(w_ready, 1)
            dve.wait_ge(b_in, 16 * (QK_CHUNKS + 1))
            with dve.Fori(0, B) as b:
                with dve.Fori(0, HALVES) as half:
                    i = b * HALVES + half
                    norm_tiles(nc, dve, N, T.X, i * TPB, i)
                    norm_split(nc, dve, N, lambda j: hT[:, 0, j, :], lambda j: hT[:, 1, j, :], i)

                    def third(c):
                        r = chunk_rows(c)
                        dve.wait_ge(second_ready, i * QK_CHUNKS + c + 1)
                        nc.vector.tensor_tensor(thirds[c][0:r, 2, :], rest[c][0:r, :], thirds[c][0:r, 1, :],
                                                ALU.subtract).then_inc(thirds_ready, 1)

                    for c in range(QK_CHUNKS):
                        r = chunk_rows(c)
                        dve.wait_ge(first_ready, i * QK_CHUNKS + c + 1)
                        nc.vector.scalar_tensor_tensor(out=rest[c][0:r, :], in0=psQ[c % 2][0:r, :],
                                                       scalar=bqk[0:r, c:c + 1], in1=thirds[c][0:r, 0, :],
                                                       op0=ALU.add, op1=ALU.subtract
                                                       ).then_inc(rest_ready, 1)
                        if c:
                            third(c - 1)
                    third(QK_CHUNKS - 1)
                    for t in range(TPB):
                        dve.wait_ge(v_ready, i * TPB + t + 1)
                        dst = T.V[:, ds(b * GPB, GPB), ds(half * TPB + t, 1), :].rearrange(
                            "p g o (j d) -> p (g o) j d", j=HG)[:, :, :, 0:D]
                        nc.vector.tensor_tensor(dst, psV[t % 2][:, 0:C].rearrange("p (g j d) -> p g j d", g=GPB, j=HG),
                                                bv[:].rearrange("p (g j d) -> p g j d", g=GPB, j=HG),
                                                ALU.add).then_inc(v_out, 1)

        @block.tensor
        def _(pe):
            pe.wait_ge(w_ready, 1)
            with pe.Fori(0, NBLK) as i:
                norm_transposes(nc, pe, N, T, psT, i)
                pe.wait_ge(N.parts_ready, i + 1)
                for c in range(QK_CHUNKS):
                    r = chunk_rows(c)
                    c0 = c * CHUNK_HEADS * D
                    if c >= 2:
                        pe.wait_ge(rest_ready, i * QK_CHUNKS + c - 1)
                    n = 0
                    for k in range(KC):
                        for wp, hp in PARTS:
                            last = nc.tensor.matmul(psQ[c % 2][0:r, :], w[:, wp, k, c0:c0 + r], hT[:, hp, k, :],
                                                    start=(n == 0), stop=(n == 3 * KC - 1))
                            n += 1
                    last.then_inc(qk_ready, 1)
                for t in range(TPB):
                    pe.wait_ge(v_out, i * TPB + t + 1)
                    n = 0
                    for k in range(KC):
                        for wp, hp in PARTS:
                            last = nc.tensor.matmul(psV[t % 2][:, 0:C], hT[:, hp, k, t * P:(t + 1) * P],
                                                    w[:, wp, k, 2 * C:3 * C], start=(n == 0), stop=(n == 3 * KC - 1))
                            n += 1
                    last.then_inc(v_ready, 1)
                pe.wait_ge(rest_ready, i * QK_CHUNKS + QK_CHUNKS)


SLOTS = 3
STEPS = HALVES * KT
ITEMS = HG * KT * 2
PER_STEP = [5] * 8 + [4] * 6 + [0, 0]
MAX_FIRST = [sum(PER_STEP[:s]) for s in range(STEPS)]
TURN_STEP = STEPS - 2
OUT_STEP = KT + 2


def attention_stage(nc, T, l):
    with ExitStack() as ctx:
        sb, banks, sem = scopes(nc, ctx, f"att{l}")
        QS = [sb(f"QS{s}", [P, HG, SEQ], BF16) for s in range(SLOTS)]
        KS = [sb(f"KS{s}", [P, HG, SEQ], BF16) for s in range(SLOTS)]
        VG = [sb(f"VG{s}", [P, KT, HG * 32], F32) for s in range(SLOTS)]
        PR = [sb(f"probs{s}", [P, HG, BLK], F32) for s in range(2)]
        mx = sb("mx", [P, HG * KT, 2], F32)
        negm = sb("neg_max", [P, HG * KT], F32)
        mrow = sb("neg_max_rows", [HG * KT, 2, P], BF16)
        OZ = [sb(f"OZ{s}", [P, BLK], F32) for s in range(HALVES)]
        RZ = [sb(f"RZ{s}", [P, BLK], F32) for s in range(HALVES)]
        ON = [sb(f"ON{s}", [P, BLK], F32) for s in range(HALVES)]
        psS = banks("scores", 2, width=2)
        psM = banks("for_max", 2)
        psO = banks("out", HALVES)

        ones_ready = sem("ones_ready")
        loaded = [sem(f"loaded{s}") for s in range(SLOTS)]
        m_loaded = [sem(f"m_loaded{s}") for s in range(SLOTS)]
        scores_ready = sem("scores_ready")
        exp_done = sem("exp_done")
        pv_done = sem("pv_done")
        row_ready = sem("row_ready")
        row_read = sem("row_read")
        negm_ready = sem("negm_ready")
        mT_ready = sem("mT_ready")
        mhi_ready = sem("mhi_ready")
        mrow_ready = sem("mrow_ready")
        oz_ready = sem("oz_ready")
        z_ready = sem("z_ready")
        rz_ready = sem("rz_ready")
        on_ready = sem("on_ready")
        o_stored = [sem(f"o_stored{n}") for n in range(HALVES)]
        LOADS = 16 * (2 * len(Q_TERMS) + 1)

        def over_groups(eng, body):
            whole = (GROUPS - 2) // SLOTS
            with eng.Fori(0, whole) as it:
                for s in range(SLOTS):
                    body(it * SLOTS + s, s, it, True)
            body(GROUPS - 2, (GROUPS - 2) % SLOTS, (GROUPS - 2) // SLOTS, True)
            body(GROUPS - 1, (GROUPS - 1) % SLOTS, (GROUPS - 1) // SLOTS, False)

        def next_of(s, use):
            return (s + 1) % SLOTS, use + (s + 1) // SLOTS

        block = ctx.enter_context(nc.Block())

        @block.sync
        def _(sp):
            def load(g, s):
                for n, (q, k) in enumerate(zip(Q_TERMS, K_TERMS)):
                    for dst, which, term in ((QS[s], 0, q), (KS[s], 1, k)):
                        src = T.qk_scr[g:g + 1, which, term] if isinstance(g, int) else T.qk_scr[ds(g, 1), which, term]
                        sp.dma_start(dst[n * D:(n + 1) * D, :, :], src.rearrange("o (j d) n -> d (o j) n", j=HG)
                                     ).then_inc(loaded[s], 16)
                src = T.V[:, g] if isinstance(g, int) else T.V[:, ds(g, 1)].rearrange("p o k n -> p (o k) n")
                sp.dma_start(VG[s][:], src).then_inc(loaded[s], 16)

            def store_max(g, s):
                sp.wait_ge(mrow_ready, g + 2)
                for e in range(2):
                    sp.dma_start(QS[s][ROWS + e:ROWS + e + 1, :, :], mrow[:, e, :]).then_inc(m_loaded[s], 16)

            def store_out(g, half):
                sp.wait_ge(on_ready, g * 2 + half + 3)
                dst = T.o_scr[g:g + 1, :, half * BLK:(half + 1) * BLK] if isinstance(g, int) else \
                    T.o_scr[ds(g, 1), :, half * BLK:(half + 1) * BLK]
                sp.dma_start(dst.rearrange("o p n -> (o p) n"), ON[half][:]).then_inc(o_stored[half], 16)

            sp.wait_ge(ones_ready, 2 * SLOTS)
            for g in range(SLOTS):
                load(g, g)
            store_max(0, 0)

            for g in range(GROUPS):
                store_out(g, 0)
                if g + 1 < GROUPS:
                    store_max(g + 1, (g + 1) % SLOTS)
                store_out(g, 1)
                if g + SLOTS < GROUPS:
                    sp.wait_ge(pv_done, g * STEPS + STEPS + 2)
                    load(g + SLOTS, g % SLOTS)
            for n in range(HALVES):
                sp.wait_ge(o_stored[n], 16 * (GROUPS + 1))

        @block.gpsimd
        def _(pool):
            for s in range(SLOTS):
                nc.gpsimd.memset(KS[s][96:P, :, :], 1.0).then_inc(ones_ready, 1)
                nc.gpsimd.memset(QS[s][96:P, :, :], 0.0).then_inc(ones_ready, 1)
            pool.sem_inc(on_ready, 2)
            for n in range(HALVES):
                pool.sem_inc(o_stored[n], 16)
            with pool.Fori(0, GROUPS) as g:
                for half in range(HALVES):
                    pool.wait_ge(rz_ready, g * 2 + half + 3)
                    pool.wait_ge(o_stored[half], (g + 1) * 16)
                    nc.gpsimd.tensor_tensor(ON[half][:], OZ[half][:], RZ[half][:], ALU.mult).then_inc(on_ready, 1)

        @block.scalar
        def _(act):
            act.sem_inc(exp_done, 2)

            def finish(g, half):
                act.wait_ge(pv_done, g * STEPS + (half + 1) * KT + 2)
                act.wait_ge(on_ready, g * 2 + half + 1)
                nc.scalar.activation(OZ[half][:], psO[half][:], ACT.Copy).then_inc(oz_ready, 1)

            def body(g, s, use, more):
                for st in range(STEPS):
                    act.wait_ge(pv_done, g * STEPS + st + 1)
                    for pr in range(2):
                        act.wait_ge(scores_ready, g * (2 * STEPS) + 2 * st + pr + 1)
                        nc.scalar.activation(PR[st % 2][:, 2 * pr:2 * pr + 2, :], psS[pr][:], ACT.Exp, scale=SCALE
                                             ).then_inc(exp_done, 1)
                    if st == OUT_STEP - 1:
                        finish(g, 0)
                finish(g, 1)

            with act.Fori(0, GROUPS) as g:
                body(g, None, None, True)

        @block.vector
        def _(dve):
            dve.sem_inc(row_read, 2)
            dve.sem_inc(mrow_ready, 1)
            dve.sem_inc(rz_ready, 2)

            def reduce(g, m):
                dve.wait_ge(row_ready, g * ITEMS + m + 1)
                nc.vector.tensor_reduce(mx[:, m // 2, m % 2:m % 2 + 1], psM[m % 2][:], AX_X, ALU.max
                                        ).then_inc(row_read, 1)

            def combine(g):
                dve.wait_ge(row_read, (g + 1) * ITEMS + 2)
                nc.vector.tensor_reduce(negm[:], mx[:], AX_X, ALU.max, negate=True).then_inc(negm_ready, 1)

            def rows_out(g, before):
                dve.wait_ge(mT_ready, g + 1)
                if before:
                    dve.wait_ge(m_loaded[before[0]], 32 * (before[1] + 1))
                nc.vector.tensor_copy(mrow[:, 0, :], psM[0][0:HG * KT, 0:P]).then_inc(mhi_ready, 1)
                dve.wait_ge(mhi_ready, g + 1)
                nc.vector.tensor_tensor(mrow[:, 1, :], psM[0][0:HG * KT, 0:P], mrow[:, 0, :], ALU.subtract
                                        ).then_inc(mrow_ready, 1)

            def recip(g, half):
                dve.wait_ge(z_ready, g * 2 + half + 1)
                dve.wait_ge(on_ready, g * 2 + half + 1)
                nc.vector.reciprocal(RZ[half][:], psO[half][:]).then_inc(rz_ready, 1)

            for m in range(ITEMS):
                reduce(0, m)
            combine(0)
            rows_out(0, None)

            def body(g, s, use, more):
                for st in range(STEPS):
                    if more:
                        for m in range(MAX_FIRST[st], MAX_FIRST[st] + PER_STEP[st]):
                            reduce(g + 1, m)
                        if st == TURN_STEP - 1:
                            combine(g + 1)
                        if st == TURN_STEP:
                            rows_out(g + 1, (s, use))
                    if st == OUT_STEP:
                        recip(g, 0)
                recip(g, 1)

            over_groups(dve, body)

        @block.tensor
        def _(pe):
            pe.sem_inc(pv_done, 2)

            def max_item(g, s, m):
                j, t, half = m // (2 * KT), m // 2 % KT, m % 2
                pe.wait_ge(row_read, g * ITEMS + m + 1)
                nc.tensor.matmul(psM[m % 2][:], QS[s][0:ROWS, j, t * P:(t + 1) * P],
                                 KS[s][0:ROWS, j, half * BLK:(half + 1) * BLK], start=True, stop=True
                                 ).then_inc(row_ready, 1)

            def turn(g):
                pe.wait_ge(negm_ready, g + 1)
                nc.tensor.transpose(psM[0][0:HG * KT, 0:P], negm[:], T.ident[:]).then_inc(mT_ready, 1)

            def scores(g, s, st):
                half, k = divmod(st, KT)
                for pr in range(2):
                    pe.wait_ge(exp_done, g * (2 * STEPS) + 2 * st + pr + 1)
                    for j in (2 * pr, 2 * pr + 1):
                        last = nc.tensor.matmul(psS[pr][:, j % 2, :], KS[s][0:ROWS + 2, j, k * P:(k + 1) * P],
                                                QS[s][0:ROWS + 2, j, half * BLK:(half + 1) * BLK],
                                                start=True, stop=True)
                    last.then_inc(scores_ready, 1)

            def weigh(g, s, st):
                half, k = divmod(st, KT)
                if k == 0:
                    pe.wait_ge(rz_ready, g * 2 + half + 1)
                pe.wait_ge(exp_done, g * (2 * STEPS) + 2 * st + 4)
                for j in range(HG):
                    last = nc.tensor.matmul(psO[half][32 * j:32 * j + 32, :], VG[s][:, k, 32 * j:32 * j + 32],
                                            PR[st % 2][:, j, :], start=(k == 0), stop=(k == KT - 1),
                                            tile_position=(0, 32 * j))
                last.then_inc(pv_done, 1)

            def spread(g, half):
                pe.wait_ge(oz_ready, g * 2 + half + 1)
                nc.tensor.matmul(psO[half][:], T.sel[:], OZ[half][:], start=True, stop=True).then_inc(z_ready, 1)

            pe.wait_ge(loaded[0], LOADS)
            for m in range(ITEMS):
                max_item(0, 0, m)
            turn(0)

            def body(g, s, use, more):
                ns, nuse = next_of(s, use)
                pe.wait_ge(m_loaded[s], 32 * (use + 1))
                if more:
                    pe.wait_ge(loaded[ns], LOADS * (nuse + 1))
                    pe.wait_ge(mrow_ready, g + 2)
                for st in range(STEPS):
                    scores(g, s, st)
                    if more:
                        if st == TURN_STEP:
                            turn(g + 1)
                        for m in range(MAX_FIRST[st], MAX_FIRST[st] + PER_STEP[st]):
                            max_item(g + 1, ns, m)
                    if st:
                        weigh(g, s, st - 1)
                    if st == OUT_STEP:
                        spread(g, 0)
                weigh(g, s, STEPS - 1)
                spread(g, 1)

            over_groups(pe, body)


def project_stage(nc, T, l, W, moe):
    with ExitStack() as ctx:
        sb, banks, sem = scopes(nc, ctx, f"proj{l}")
        wp = sb("w_proj", [P, GPB, C], F32)
        oT = sb("oT", [P, GPB, BLK], F32)
        upd = sb("update", [P, TPB, C], F32)
        N = Norm(sb, sem)
        psT = banks("xT", KC)
        psP = banks("proj", 2)
        psL = banks("logits", 1)[0]
        psLT = banks("logitsT", 1)[0]

        w_zero = sem("w_zero")
        w_in = sem("w_in")
        o_in = sem("o_in")
        proj_ready = sem("proj_ready")
        gated = sem("gated")
        added = sem("added")
        wg_in = sem("wg_in")
        wg_zero = sem("wg_zero")
        wghi_ready = sem("wghi_ready")
        wg_ready = sem("wg_ready")
        lg_ready = sem("lg_ready")
        lg_copied = sem("lg_copied")
        lgT_ready = sem("lgT_ready")
        lgT_read = sem("lgT_read")
        chain = sem("route_steps")
        ex_ready = sem("ex_ready")
        if moe:
            wgs = sb("w_gate_f32", [CK, KC, P], F32)
            wg = sb("w_gate_parts", [CK, 2, KC, P], F32R)
            lg = sb("logits_sb", [E, BLK], F32)
            LG = sb("logits_all", [P, TILES, E], F32)
            rank = sb("rank", [P, TILES, E], F32)
            cmp = sb("cmp", [P, TILES], F32)
            top = sb("top", [P, TILES], F32)
            ex = sb("ex", [P, TILES, E], F32)
            den = sb("den", [P, TILES], F32)

        block = ctx.enter_context(nc.Block())

        @block.sync
        def _(sp):
            sp.wait_ge(w_zero, 1)
            for j in range(HG):
                for g in range(GPB):
                    h = g * HG + j
                    sp.dma_start(wp[32 * j:32 * j + D, g, :], W.w_proj[h * D:(h + 1) * D, :]).then_inc(w_in, 16)
            sp.dma_start(wp[D:D + 1, 0, :], row(W.b_proj, 1)).then_inc(w_in, 16)
            if moe:
                sp.wait_ge(wg_zero, 1)
                sp.dma_start(wgs[:, :, 0:E], W.w_gate.rearrange("(k p) n -> p k n", p=CK)).then_inc(wg_in, 16)
            with sp.Fori(0, B) as b:
                with sp.Fori(0, HALVES) as half:
                    i = b * HALVES + half
                    sp.wait_ge(proj_ready, i * TPB + 1)
                    sp.dma_start(oT[:], T.o_scr[ds(b * GPB, GPB), :, ds(half * BLK, BLK)].rearrange("g p n -> p g n")
                                 ).then_inc(o_in, 16)

        @block.gpsimd
        def _(pool):
            nc.gpsimd.memset(wp[:], 0.0).then_inc(w_zero, 1)
            if moe:
                nc.gpsimd.memset(wgs[:], 0.0).then_inc(wg_zero, 1)

        @block.scalar
        def _(act):
            with act.Fori(0, B) as b:
                with act.Fori(0, HALVES) as half:
                    i = b * HALVES + half
                    norm_modulate(nc, act, N, T.mod[l], 2, psT, b, i)
                    if moe:
                        act.wait_ge(lg_ready, i + 1)
                        nc.scalar.activation(lg[:], psL[0:E, :], ACT.Copy).then_inc(lg_copied, 1)
            if moe:
                act.wait_ge(chain, 2)
                nc.scalar.activation(ex[:], ex[:], ACT.Exp).then_inc(ex_ready, 1)

        @block.vector
        def _(dve):
            if moe:
                dve.wait_ge(wg_in, 16)
                nc.vector.tensor_copy(wg[:, 0], wgs[:]).then_inc(wghi_ready, 1)
                dve.wait_ge(wghi_ready, 1)
                nc.vector.tensor_tensor(wg[:, 1], wgs[:], wg[:, 0].bitcast(F32), ALU.subtract).then_inc(wg_ready, 1)
            with dve.Fori(0, B) as b:
                with dve.Fori(0, HALVES) as half:
                    i = b * HALVES + half
                    for t in range(TPB):
                        dve.wait_ge(proj_ready, i * TPB + t + 2)
                        nc.vector.tensor_tensor(upd[:, t, :], psP[t % 2][:, 0:C],
                                                T.gate[l][:, 0, ds(b, 1), :].rearrange("p o c -> p (o c)"), ALU.mult
                                                ).then_inc(gated, 1)
                    dve.wait_ge(gated, i * TPB + TPB)
                    x = T.X[:, ds(i * TPB, TPB), :]
                    nc.vector.tensor_tensor(x, x, upd[:], ALU.add).then_inc(added, 1)
                    wait_alone(dve, added, i + 1, N.passed)
                    norm_tiles(nc, dve, N, T.X, i * TPB, i)
                    norm_split(nc, dve, N, lambda j: T.hT[:, 0, j, ds(i * BLK, BLK)],
                               lambda j: T.hT[:, 1, j, ds(i * BLK, BLK)], i)
                    if moe:
                        dve.wait_ge(lgT_ready, i + 1)
                        nc.vector.tensor_copy(LG[:, ds(i * TPB, TPB), :],
                                              psLT[:, 0:TPB * E].rearrange("p (t e) -> p t e", e=E)
                                              ).then_inc(lgT_read, 1)
            if not moe:
                return
            dve.wait_ge(lgT_read, NBLK)
            n = 0

            def step(ins):
                nonlocal n
                n += 1
                ins.then_inc(chain, 1)
                dve.wait_ge(chain, n)

            step(nc.vector.tensor_reduce(top[:], LG[:], AX_X, ALU.max))
            step(nc.vector.tensor_tensor(ex[:], LG[:], top[:].rearrange("p (t o) -> p t o", o=1).broadcast_to([P, TILES, E]),
                                         ALU.subtract))
            step(nc.vector.memset(rank[:], 0.0))
            for a in range(E):
                for c in range(a + 1, E):
                    step(nc.vector.tensor_tensor(cmp[:], LG[:, :, a], LG[:, :, c], ALU.is_ge))
                    step(nc.vector.tensor_tensor(rank[:, :, c], rank[:, :, c], cmp[:], ALU.add))
                    step(nc.vector.scalar_tensor_tensor(out=rank[:, :, a], in0=rank[:, :, a], scalar=1.0, in1=cmp[:],
                                                        op0=ALU.add, op1=ALU.subtract))
            step(nc.vector.tensor_scalar(rank[:], rank[:], 2.0, None, ALU.is_lt))
            dve.wait_ge(ex_ready, 1)
            step(nc.vector.tensor_tensor(ex[:], ex[:], rank[:], ALU.mult))
            step(nc.vector.reduce_sum(den[:], ex[:], AX_X))
            step(nc.vector.reciprocal(den[:], den[:]))
            step(nc.vector.tensor_tensor(T.cw[:], ex[:], den[:].rearrange("p (t o) -> p t o", o=1).broadcast_to([P, TILES, E]),
                                         ALU.mult))

        @block.tensor
        def _(pe):
            pe.sem_inc(proj_ready, 1)
            pe.wait_ge(w_in, 16 * (H + 1))
            if moe:
                pe.wait_ge(wg_ready, 1)
            with pe.Fori(0, NBLK) as i:
                pe.wait_ge(o_in, (i + 1) * 16)
                for t in range(TPB):
                    if t >= 2:
                        pe.wait_ge(gated, i * TPB + t - 1)
                    for g in range(GPB):
                        last = nc.tensor.matmul(psP[t % 2][:, 0:C], oT[:, g, t * P:(t + 1) * P], wp[:, g, :],
                                                start=(g == 0), stop=(g == GPB - 1))
                    last.then_inc(proj_ready, 1)
                norm_transposes(nc, pe, N, T, psT, i)
                pe.wait_ge(N.parts_ready, i + 1)
                if moe:
                    n = 0
                    for k in range(KC):
                        for wpart, hpart in PARTS:
                            last = nc.tensor.matmul(psL[:], wg[:, wpart, k, :], T.hT[:, hpart, k, ds(i * BLK, BLK)],
                                                    start=(n == 0), stop=(n == 3 * KC - 1))
                            n += 1
                    last.then_inc(lg_ready, 1)
                    wait_alone(pe, lg_copied, i + 1, N.passed)
                    for t in range(TPB):
                        last = nc.tensor.transpose(psLT[:, t * E:(t + 1) * E], lg[:, t * P:(t + 1) * P],
                                                   T.ident[0:E, 0:E])
                    last.then_inc(lgT_ready, 1)
                    pe.wait_ge(lgT_read, i + 1)


def mlp_stage(nc, T, l, W, experts):
    with ExitStack() as ctx:
        sb, banks, sem = scopes(nc, ctx, f"mlp{l}")
        SETS = min(2, experts)
        RING = 3
        st1 = sb("w1_f32", [CK, FF], F32)
        st2 = sb("w2_f32", [P, 3, C], F32)
        w1 = [sb(f"w1_parts{s}", [CK, 2, KC, FF], F32R) for s in range(SETS)]
        w2 = [sb(f"w2_parts{s}", [P, 2, NF, C], F32R) for s in range(SETS)]
        b1 = [sb(f"b1_{s}", [P, NF], F32) for s in range(SETS)]
        b2 = [sb(f"b2_{s}", [P, C], F32) for s in range(SETS)]
        g32 = [sb(f"gelu{n}", [P, BLK], F32) for n in range(RING)]
        hp = [sb(f"hidden_parts{n}", [P, 2, BLK], F32R) for n in range(RING)]
        upd = sb("update", [P, TPB, C], F32)
        psH = banks("hidden", RING)
        psY = banks("y", TPB)

        passed = sem("waits_passed")
        st1_in = sem("st1_in")
        st2_in = sem("st2_in")
        st1_used = sem("st1_used")
        st2_used = sem("st2_used")
        bias_in = [sem(f"bias_in{s}") for s in range(SETS)]
        whi = sem("w_hi_ready")
        w_ready = sem("w_ready")
        expert_done = sem("expert_done")
        bias_used = sem("bias_used")
        h_ready = sem("h_ready")
        gelu_ready = sem("gelu_ready")
        hi_ready = sem("hi_ready")
        parts_ready = sem("parts_ready")
        used = sem("hidden_used")
        y_ready = sem("y_ready")
        y_read = sem("y_read")
        steps = sem("update_steps")

        def over_experts(eng, body):
            if experts == 1:
                body(0, 0, 0)
            else:
                with eng.Fori(0, experts // SETS) as it:
                    for s in range(SETS):
                        body(it * SETS + s, s, it)

        def pick(ap, e):
            return ap[e] if isinstance(e, int) else ap[ds(e, 1)].squeeze(0)

        block = ctx.enter_context(nc.Block())

        @block.sync
        def _(sp):
            def body(e, s, use):
                v1 = pick(W.w1, e).rearrange("(k p) n -> k p n", p=CK)
                v2 = pick(W.w2, e).rearrange("(f p) n -> p f n", p=P)
                for k in range(KC):
                    sp.wait_ge(st1_used, e * KC + k + 1)
                    sp.dma_start(st1[:], v1[k]).then_inc(st1_in, 16)
                    sp.wait_ge(st2_used, e * KC + k + 1)
                    sp.dma_start(st2[:], v2[:, 3 * k:3 * k + 3, :]).then_inc(st2_in, 16)
                sp.wait_ge(bias_used, e + 1)
                sp.dma_start(b1[s][:], pick(W.b1, e).rearrange("(f p) -> p f", p=P),
                             allow_slow_non_contiguous=True).then_inc(bias_in[s], 16)
                sp.dma_start(b2[s][:], row(pick(W.b2, e), P)).then_inc(bias_in[s], 16)

            over_experts(sp, body)

        @block.gpsimd
        def _(pool):
            pool.sem_inc(st1_used, 1)
            pool.sem_inc(st2_used, 1)

            def body(e, s, use):
                pool.wait_ge(expert_done, e + 1)
                for k in range(KC):
                    wait_alone(pool, st1_in, e * (16 * KC) + 16 * (k + 1), passed)
                    nc.gpsimd.tensor_copy(w1[s][:, 0, k, :], st1[:]).then_inc(whi, 1)
                    pool.wait_ge(whi, e * (2 * KC) + 2 * k + 1)
                    nc.gpsimd.tensor_tensor(w1[s][:, 1, k, :], st1[:], w1[s][:, 0, k, :].bitcast(F32), ALU.subtract
                                            ).then_inc(st1_used, 1)
                    wait_alone(pool, st2_in, e * (16 * KC) + 16 * (k + 1), passed)
                    nc.gpsimd.tensor_copy(w2[s][:, 0, 3 * k:3 * k + 3, :], st2[:]).then_inc(whi, 1)
                    pool.wait_ge(whi, e * (2 * KC) + 2 * k + 2)
                    nc.gpsimd.tensor_tensor(w2[s][:, 1, 3 * k:3 * k + 3, :], st2[:],
                                            w2[s][:, 0, 3 * k:3 * k + 3, :].bitcast(F32), ALU.subtract
                                            ).then_inc(st2_used, 1)

            over_experts(pool, body)

        @block.scalar
        def _(act):
            def body(e, s, use):
                act.wait_ge(bias_in[s], (use + 1) * 32)
                with act.Fori(0, NBLK) as i:
                    at = (e * NBLK + i) * NF
                    for f in range(NF):
                        act.wait_ge(h_ready, at + f + 1)
                        act.wait_ge(parts_ready, at + f + 1)
                        nc.scalar.activation(g32[f % RING][:], psH[f % RING][:], ACT.Gelu_apprx_tanh,
                                             bias=b1[s][:, f:f + 1]).then_inc(gelu_ready, 1)

            over_experts(act, body)

        @block.vector
        def _(dve):
            dve.sem_inc(parts_ready, RING)
            dve.sem_inc(y_read, TPB)
            dve.sem_inc(bias_used, SETS)

            def body(e, s, use):
                wait_alone(dve, bias_in[s], (use + 1) * 32, passed)
                with dve.Fori(0, B) as b:
                    with dve.Fori(0, HALVES) as half:
                        i = b * HALVES + half
                        n = e * NBLK + i
                        for f in range(NF):
                            dve.wait_ge(gelu_ready, n * NF + f + 1)
                            dve.wait_ge(used, n * NF + f + 1)
                            nc.vector.tensor_copy(hp[f % RING][:, 0, :], g32[f % RING][:]).then_inc(hi_ready, 1)
                            dve.wait_ge(hi_ready, n * NF + f + 1)
                            nc.vector.tensor_tensor(hp[f % RING][:, 1, :], g32[f % RING][:],
                                                    hp[f % RING][:, 0, :].bitcast(F32), ALU.subtract
                                                    ).then_inc(parts_ready, 1)
                        for t in range(TPB):
                            dve.wait_ge(y_ready, n * TPB + t + 1)
                            nc.vector.tensor_tensor(upd[:, t, :], psY[t][:, 0:C], b2[s][:], ALU.add
                                                    ).then_inc(y_read, 1)
                        dve.wait_ge(y_read, n * TPB + 2 * TPB)
                        for t in range(TPB):
                            last = nc.vector.tensor_tensor(upd[:, t, :], upd[:, t, :],
                                                           T.gate[l][:, 1, ds(b, 1), :].rearrange("p o c -> p (o c)"),
                                                           ALU.mult)
                        last.then_inc(steps, 1)
                        dve.wait_ge(steps, n * 2 + 1)
                        for t in range(TPB):
                            x = T.X[:, ds(i * TPB + t, 1), :].rearrange("p o c -> p (o c)")
                            weight = 1.0 if experts == 1 else \
                                T.cw[:, ds(i * TPB + t, 1), ds(e, 1)].rearrange("p t e -> p (t e)")
                            last = nc.vector.scalar_tensor_tensor(out=x, in0=upd[:, t, :], scalar=weight, in1=x,
                                                                  op0=ALU.mult, op1=ALU.add)
                        last.then_inc(steps, 1)
                        dve.wait_ge(steps, n * 2 + 2)
                dve.sem_inc(bias_used, 1)

            over_experts(dve, body)

        @block.tensor
        def _(pe):
            pe.sem_inc(expert_done, SETS)
            pe.sem_inc(used, RING)

            def body(e, s, use):
                pe.wait_ge(st1_used, e * KC + KC + 1)
                wait_alone(pe, st2_used, e * KC + KC + 1, passed)
                with pe.Fori(0, NBLK) as i:
                    blk = e * NBLK + i

                    def up(f):
                        pe.wait_ge(parts_ready, blk * NF + f + 1)
                        n = 0
                        for k in range(KC):
                            for wpart, hpart in PARTS:
                                last = nc.tensor.matmul(psH[f % RING][:], w1[s][:, wpart, k, f * P:(f + 1) * P],
                                                        T.hT[:, hpart, k, ds(i * BLK, BLK)],
                                                        start=(n == 0), stop=(n == 3 * KC - 1))
                                n += 1
                        last.then_inc(h_ready, 1)

                    def down(f):
                        pe.wait_ge(parts_ready, blk * NF + f + 1 + RING)
                        for t in range(TPB):
                            if f == 0:
                                pe.wait_ge(y_read, blk * TPB + t + 1)
                            for n, (wpart, hpart) in enumerate(PARTS):
                                last = nc.tensor.matmul(psY[t][:, 0:C], hp[f % RING][:, hpart, t * P:(t + 1) * P],
                                                        w2[s][:, wpart, f, :], start=(f == 0 and n == 0),
                                                        stop=(f == NF - 1 and n == 2))
                            if f == NF - 1:
                                last.then_inc(y_ready, 1)
                        if f < NF - 1:
                            last.then_inc(used, 1)

                    for f in range(NF):
                        up(f)
                        if f:
                            down(f - 1)
                    down(NF - 1)
                    pe.wait_ge(y_ready, blk * TPB + TPB)
                    pe.sem_inc(used, 1)
                pe.sem_inc(expert_done, 1)

            over_experts(pe, body)


def store_stage(nc, T, out):
    with ExitStack() as ctx:
        _, _, sem = scopes(nc, ctx, "store")
        stored = sem("stored")
        block = ctx.enter_context(nc.Block())

        @block.sync
        def _(sp):
            sp.dma_start(out.rearrange("b (t p) c -> p (b t) c", p=P), T.X[:]).then_inc(stored, 16)
            sp.wait_ge(stored, 16)


class Shared:
    pass


class Layer:

    def __init__(self, A, prefix, w_ada, b_ada, w_qkv, w_proj, w1, b1, w2, b2):
        self.w_ada, self.b_ada = A[prefix + w_ada], A[prefix + b_ada]
        self.w_qkv, self.b_qkv = A[prefix + w_qkv], A[prefix + "b_qkv"]
        self.w_proj, self.b_proj = A[prefix + w_proj], A[prefix + "b_proj"]
        self.w1, self.b1, self.w2, self.b2 = (A[prefix + n] for n in (w1, b1, w2, b2))
        if len(self.w1.shape) == 2:
            self.w1 = self.w1.rearrange("(o c) n -> o c n", o=1)
            self.b1 = self.b1.rearrange("(o c) -> o c", o=1)
            self.w2 = self.w2.rearrange("(o c) n -> o c n", o=1)
            self.b2 = self.b2.rearrange("(o c) -> o c", o=1)


def program(nc, A, out):
    layers = [Layer(A, "L0_cond_", "W_ada", "b_ada", "W_qkv", "W_proj", "W_fc1", "b_fc1", "W_fc2", "b_fc2"),
              Layer(A, "L1_cond_", "w_adaln", "b_adaln", "w_qkv", "w_proj", "w1", "b1", "w2", "b2")]
    layers[1].w_gate = A["L1_cond_w_gate"]
    with ExitStack() as ctx:
        sb = lambda name, shape, dt: ctx.enter_context(nc.sbuf_tensor(name, shape, dt))
        T = Shared()
        T.X = sb("X", [P, TILES, C], F32)
        T.ident = sb("ident", [P, P], F32)
        T.mod = [sb(f"mod{l}", [CK, 4, KC, B], F32) for l in range(2)]
        T.gate = [sb(f"gate{l}", [P, 2, B, C], F32) for l in range(2)]
        T.cw = sb("expert_weights", [P, TILES, E], F32)
        T.sel = sb("sel", [P, P], F32)
        T.qk_scr = nc.dram_tensor("qk_thirds", (GROUPS, 2, 3, HG * D, SEQ), BF16).ap()
        T.o_scr = nc.dram_tensor("heads_out", (GROUPS, P, SEQ), F32).ap()
        modulation(nc, T, A["x"], A["cond_1152"], layers)
        selection(nc, T)
        for l, W in enumerate(layers):
            with ExitStack() as scope:
                T.V = scope.enter_context(nc.sbuf_tensor(f"V{l}", [P, GROUPS, KT, HG * 32], F32))
                qkv_stage(nc, T, l, W)
                attention_stage(nc, T, l)
            with ExitStack() as scope:
                T.hT = scope.enter_context(nc.sbuf_tensor(f"hT{l}", [CK, 2, KC, TOKENS], F32R))
                project_stage(nc, T, l, W, moe=(l == 1))
                mlp_stage(nc, T, l, W, experts=(1, E)[l])
        store_stage(nc, T, out)


def selection(nc, T):
    with ExitStack() as ctx:
        _, _, sem = scopes(nc, ctx, "sel")
        zeroed = sem("zeroed")
        block = ctx.enter_context(nc.Block())

        @block.gpsimd
        def _(pool):
            nc.gpsimd.memset(T.sel[:], 0.0).then_inc(zeroed, 1)
            pool.wait_ge(zeroed, 1)
            v = T.sel[:].rearrange("p (j d) -> p j d", j=HG)
            nc.gpsimd.affine_select(out=v, in_=v, compare_op=ALU.not_equal, fill=1.0, base=-D,
                                    pattern=[[-32, HG], [0, 32]], channel_multiplier=1).then_inc(zeroed, 1)
            pool.wait_ge(zeroed, 2)


_INS = ['x', 'cond_1152', 'L0_cond_W_qkv', 'L0_cond_b_qkv', 'L0_cond_W_proj', 'L0_cond_b_proj', 'L0_cond_W_fc1',
        'L0_cond_b_fc1', 'L0_cond_W_fc2', 'L0_cond_b_fc2', 'L0_cond_W_ada', 'L0_cond_b_ada', 'L1_cond_w_adaln',
        'L1_cond_b_adaln', 'L1_cond_w_qkv', 'L1_cond_b_qkv', 'L1_cond_w_proj', 'L1_cond_b_proj', 'L1_cond_w_gate',
        'L1_cond_w1', 'L1_cond_b1', 'L1_cond_w2', 'L1_cond_b2']


def kernel(**inputs):
    import numpy as _np
    import concourse.bacc as _bacc
    from concourse import mybir as _mybir
    from concourse.bass_utils import run_bass_kernel_spmd as _run

    nc = _bacc.Bacc("TRN2", target_bir_lowering=False, num_devices=1)
    arrays, args = {}, {}
    for name in _INS:
        a = _np.ascontiguousarray(inputs[name])
        arrays[f"in_{name}_dram"] = a
        args[name] = nc.dram_tensor(f"in_{name}_dram", a.shape, _mybir.dt.from_np(a.dtype), kind="ExternalInput").ap()
    out = nc.dram_tensor("out_0_dram", (B, SEQ, C), F32, kind="ExternalOutput").ap()
    program(nc, args, out)
    r = _run(nc, [arrays], core_ids=[0])
    return r.results[0]["out_0_dram"]
```

```python
from contextlib import ExitStack

import concourse.bass as bass
from concourse import mybir

ACT = mybir.ActivationFunctionType
ALU = mybir.AluOpType
AX_X = mybir.AxisListType.X
F32 = mybir.dt.float32
F32R = mybir.dt.float32r
BF16 = mybir.dt.bfloat16
ds = bass.ds

P = 128
B, SEQ, C, H = 2, 1024, 288, 16
D = C // H
FF = 4 * C
E = 4
TOKENS = B * SEQ
TILES = TOKENS // P
FULL = C // P
REST = C - FULL * P
KC = FULL + 1
NF = FF // P
BLK = 512
TPB = BLK // P
NBLK = TOKENS // BLK
HALVES = SEQ // BLK
EPS = 1e-6
SCALE = float(D) ** -0.5
HG = 4
GPB = H // HG
GROUPS = B * GPB
KT = SEQ // P
PARTS = ((0, 0), (1, 0), (0, 1))
STACK = len(PARTS) * REST
W_LO = slice(REST, 2 * REST)
H_LO = slice(2 * REST, STACK)
HI, LO, STK = 0, FULL, 2 * FULL
SLOT = 2 * FULL + 1
PASSES = [(k + FULL * wp, k + FULL * hp, P) for k in range(FULL) for wp, hp in PARTS] + [(STK, STK, STACK)]
CX = C + STACK - REST
CHUNK = [(0, P), (P, P), (2 * P, STACK)]
Q_TERMS, K_TERMS = (0, 0, 0, 1, 1, 2), (0, 1, 2, 0, 1, 0)
ROWS = len(Q_TERMS) * D
QK_HEADS = 2 * H
CHUNK_HEADS = P // D
QK_CHUNKS = -(-QK_HEADS // CHUNK_HEADS)


def chunk_rows(c):
    return min(CHUNK_HEADS, QK_HEADS - CHUNK_HEADS * c) * D


def chunk_pieces(c):
    heads = range(CHUNK_HEADS * c, min(CHUNK_HEADS * (c + 1), QK_HEADS))
    out = []
    for n in sorted({h // HG for h in heads}):
        own = [h for h in heads if h // HG == n]
        out.append(((own[0] - heads[0]) * D, len(own) * D, n // GPB, n % GPB, own[0] % HG * D))
    return out


def load_chunks(eng, dst, src, sem):
    for k in range(FULL):
        eng.dma_start(dst(k)[:], src[k * P:(k + 1) * P]).then_inc(sem, 16)
    for n in range(len(PARTS)):
        eng.dma_start(dst(FULL)[n * REST:(n + 1) * REST], src[FULL * P:C]).then_inc(sem, 16)


CHUNK_LOADS = FULL + len(PARTS)


def row(ap, n):
    return ap.rearrange("(o c) -> o c", o=1).broadcast_to([n, ap.shape[0]])


def scopes(nc, ctx, stage):
    def sb(name, shape, dt):
        return ctx.enter_context(nc.sbuf_tensor(f"{stage}_{name}", shape, dt))

    def banks(name, n, width=1):
        shape = [P, 512] if width == 1 else [P, width, 512]
        return [ctx.enter_context(nc.psum_tensor(f"{stage}_{name}{i}", shape, F32)) for i in range(n)]

    sems = []

    @ctx.callback
    def _():
        nc.clear_and_free_semaphores(sems)
        nc.all_engine_barrier()

    def sem(name):
        sems.append(nc.alloc_semaphore(name=f"{stage}_{name}"))
        return sems[-1]

    return sb, banks, sem


def modulation(nc, T, x, cond, layers):
    with ExitStack() as ctx:
        sb, banks, sem = scopes(nc, ctx, "ada")
        CK = C // 3
        NK = C // CK
        NA = P // 32
        AW = 6 * C // NA
        cT = sb("cT", [CK, NK, B], F32)
        sc = sb("sc", [CK, NK, B], F32)
        ones = sb("ones", [B, P], F32)
        pick = sb("pick_entry", [B, B, P], F32)
        w = [sb(f"w_ada{l}", [CK, NK, 6 * C], F32) for l in range(2)]
        brow = [sb(f"b_ada_rows{l}", [B, 6 * C], F32) for l in range(2)]
        arow = [sb(f"ada_rows{l}", [B, 6 * C], F32) for l in range(2)]
        acols = [sb(f"ada_cols{l}", [B, 4, CX], F32) for l in range(2)]
        ps = banks("ada", 2)
        psT = banks("adaT", 1)[0]
        psG = banks("gateP", 2 * B)

        cond_in = sem("cond_in")
        b_in = sem("b_in")
        w_in = [sem(f"w_in{l}") for l in range(2)]
        x_in = sem("x_in")
        ident0 = sem("ident0")
        ident_ready = sem("ident_ready")
        ones_ready = sem("ones_ready")
        silu_ready = sem("silu_ready")
        pick_ready = sem("pick_ready")
        sel_zero = sem("sel_zero")
        sel_ready = sem("sel_ready")
        rows_ready = sem("rows_ready")
        rows_out = sem("rows_out")
        acols_ready = sem("acols_ready")
        cols_ready = sem("cols_ready")
        cols_out = sem("cols_out")
        gate_ready = sem("gate_ready")
        gate_out = sem("gate_out")

        block = ctx.enter_context(nc.Block())

        @block.sync
        def _(sp):
            for b in range(B):
                for j in range(NK):
                    sp.dma_start(cT[:, j, b:b + 1], cond[b, j * CK:(j + 1) * CK].rearrange("(p o) -> p o", o=1)
                                 ).then_inc(cond_in, 16)
            for l in range(2):
                sp.dma_start(brow[l][:], row(layers[l].b_ada, B)).then_inc(b_in, 16)
            for l in range(2):
                sp.dma_start(w[l][:], layers[l].w_ada.rearrange("(k p) n -> p k n", p=CK)).then_inc(w_in[l], 16)
            sp.dma_start(T.X[:], x.rearrange("b (t p) c -> p (b t) c", p=P)).then_inc(x_in, 16)
            load_w_qkv(sp, T, layers[0], x_in)
            sp.wait_ge(x_in, 16 * (1 + CHUNK_LOADS))

        @block.gpsimd
        def _(pool):
            nc.gpsimd.memset(T.ident[:], 0.0).then_inc(ident0, 1)
            pool.wait_ge(ident0, 1)
            nc.gpsimd.affine_select(out=T.ident[:], in_=T.ident[:], compare_op=ALU.not_equal, fill=1.0, base=0,
                                    pattern=[[-1, P]], channel_multiplier=1).then_inc(ident_ready, 1)
            nc.gpsimd.memset(T.sel[:], 0.0).then_inc(sel_zero, 1)
            pool.wait_ge(sel_zero, 1)
            v = T.sel[:].rearrange("p (j d) -> p j d", j=HG)
            nc.gpsimd.affine_select(out=v, in_=v, compare_op=ALU.not_equal, fill=1.0, base=-D,
                                    pattern=[[-32, HG], [0, 32]], channel_multiplier=1).then_inc(sel_ready, 1)
            pool.wait_ge(sel_ready, 1)

        @block.scalar
        def _(act):
            act.wait_ge(cond_in, 16 * B * NK)
            nc.scalar.activation(sc[:], cT[:], ACT.Silu).then_inc(silu_ready, 1)

        @block.vector
        def _(dve):
            nc.vector.memset(ones[:], 1.0).then_inc(ones_ready, 1)
            dve.wait_ge(ones_ready, 1)
            dve.wait_ge(ident_ready, 1)
            for b in range(B):
                last = nc.vector.tensor_scalar(pick[:, b, :], ones[:], T.ident[0:B, b:b + 1], None, ALU.mult)
            last.then_inc(pick_ready, 1)
            dve.wait_ge(b_in, 32)
            for l in range(2):
                dve.wait_ge(rows_ready, l + 1)
                for n in range(NA):
                    last = nc.vector.tensor_tensor(arow[l][:, n * AW:(n + 1) * AW], ps[l][32 * n:32 * n + B, 0:AW],
                                                   brow[l][:, n * AW:(n + 1) * AW], ALU.add)
                last.then_inc(rows_out, 1)
                dve.wait_ge(rows_out, l + 1)
                for n, part in enumerate((0, 1, 3, 4)):
                    c0 = part * C
                    nc.vector.tensor_scalar(acols[l][:, n, 0:FULL * P], arow[l][:, c0:c0 + FULL * P],
                                            float(n % 2), None, ALU.add)
                    tail = arow[l][:, c0 + FULL * P:c0 + C].rearrange("p (o c) -> p o c", o=1)
                    last = nc.vector.tensor_scalar(acols[l][:, n, FULL * P:CX].rearrange("p (o c) -> p o c", c=REST),
                                                   tail.broadcast_to([B, len(PARTS), REST]), float(n % 2), None, ALU.add)
                last.then_inc(acols_ready, 1)
                for g in range(2):
                    for b in range(B):
                        n = 2 * g + b
                        dve.wait_ge(gate_ready, 2 * B * l + n + 1)
                        nc.vector.tensor_copy(T.gate[l][:, g, b, :], psG[n][:, 0:C]).then_inc(gate_out, 1)
                dve.wait_ge(cols_ready, l + 1)
                for j, (_, r) in enumerate(CHUNK):
                    last = nc.vector.tensor_copy(T.mod[l][0:r, :, j], psT[0:r, j * 4 * B:(j + 1) * 4 * B].rearrange(
                        "p (n b) -> p n b", n=4))
                last.then_inc(cols_out, 1)

        @block.tensor
        def _(pe):
            pe.wait_ge(silu_ready, 1)

            def rows(l):
                pe.wait_ge(w_in[l], 16)
                for j in range(NK):
                    for n in range(NA):
                        last = nc.tensor.matmul(ps[l][32 * n:32 * n + B, 0:AW], sc[:, j, :], w[l][:, j, n * AW:(n + 1) * AW],
                                                start=(j == 0), stop=(j == NK - 1), tile_position=(0, 32 * n))
                last.then_inc(rows_ready, 1)

            for l in range(2):
                rows(l)
                pe.wait_ge(pick_ready, 1)
                pe.wait_ge(rows_out, l + 1)
                for g, part in enumerate((2, 5)):
                    for b in range(B):
                        n = 2 * g + b
                        if l:
                            pe.wait_ge(gate_out, n + 1)
                        nc.tensor.matmul(psG[n][:, 0:C], pick[:, b, :], arow[l][:, part * C:(part + 1) * C],
                                         start=True, stop=True).then_inc(gate_ready, 1)
                pe.wait_ge(acols_ready, l + 1)
                if l:
                    pe.wait_ge(cols_out, 1)
                for n in range(4):
                    for j, (c0, r) in enumerate(CHUNK):
                        at = (j * 4 + n) * B
                        last = nc.tensor.transpose(psT[0:r, at:at + B], acols[l][:, n, c0:c0 + r], T.ident[0:B, 0:B])
                last.then_inc(cols_ready, 1)


def wait_alone(eng, sem, value, passed):
    eng.wait_ge(sem, value)
    eng.sem_inc(passed, 1)


class Norm:

    def __init__(self, sb, sem):
        self.stats = sb("bn_stats", [P, TPB, 6], F32)
        self.mv = sb("mean_var", [P, TPB, 2], F32)
        self.veps = sb("var_eps", [P, TPB], F32)
        self.std = sb("std", [P, TPB], F32)
        self.rstd = sb("rstd", [P, TPB], F32)
        self.xn = sb("x_normed", [P, TPB, CX], F32)
        self.h = sb("h_mod", [P, KC, BLK], F32)
        self.steps = sem("norm_steps")
        self.passed = sem("waits_passed")
        self.var_ready = sem("var_ready")
        self.std_ready = sem("std_ready")
        self.xn_ready = sem("xn_ready")
        self.xt_ready = sem("xt_ready")
        self.h_ready = sem("h_ready")
        self.hi_ready = sem("hi_ready")
        self.parts_ready = sem("parts_ready")


def norm_variance(nc, dve, N, X, i):
    for t in range(TPB):
        last = nc.vector.bn_stats(N.stats[:, t, :], X[:, ds(i * TPB + t, 1), :].rearrange("p o c -> p (o c)"))
    last.then_inc(N.steps, 1)
    wait_alone(dve, N.steps, i * 3 + 1, N.passed)
    for t in range(TPB):
        last = nc.vector.bn_aggr(N.mv[:, t, :], N.stats[:, t, :])
    last.then_inc(N.steps, 1)
    dve.wait_ge(N.steps, i * 3 + 2)
    nc.vector.tensor_scalar(N.veps[:], N.mv[:, :, 1], EPS, None, ALU.add).then_inc(N.var_ready, 1)


def norm_tiles(nc, dve, N, X, i):
    dve.wait_ge(N.std_ready, i + 1)
    nc.vector.reciprocal(N.rstd[:], N.std[:]).then_inc(N.steps, 1)
    dve.wait_ge(N.steps, i * 3 + 3)
    dve.wait_ge(N.xt_ready, (i + 1) * KC)
    for t in range(TPB):
        x = X[:, ds(i * TPB + t, 1), :]
        again = x[:, :, FULL * P:C].broadcast_to([P, len(PARTS) - 1, REST])
        nc.vector.tensor_scalar(N.xn[:, t, 0:C], x.rearrange("p o c -> p (o c)"),
                                N.mv[:, t, 0:1], N.rstd[:, t:t + 1], ALU.subtract, ALU.mult)
        last = nc.vector.tensor_scalar(N.xn[:, t, C:CX].rearrange("p (o c) -> p o c", c=REST), again,
                                       N.mv[:, t, 0:1], N.rstd[:, t:t + 1], ALU.subtract, ALU.mult)
    last.then_inc(N.xn_ready, 1)


def norm_transposes(nc, pe, N, T, psT, i):
    pe.wait_ge(N.xn_ready, i + 1)
    for j, (c0, r) in enumerate(CHUNK):
        pe.wait_ge(N.h_ready, i * KC + j + 1)
        for t in range(TPB):
            last = nc.tensor.transpose(psT[j][0:r, t * P:(t + 1) * P], N.xn[:, t, c0:c0 + r], T.ident[:])
        last.then_inc(N.xt_ready, 1)


def norm_root(nc, act, N, i):
    act.wait_ge(N.var_ready, i + 1)
    nc.scalar.activation(N.std[:], N.veps[:], ACT.Sqrt).then_inc(N.std_ready, 1)


def norm_modulate(nc, act, N, mod, which, psT, b, i):
    for j, (_, r) in enumerate(CHUNK):
        act.wait_ge(N.xt_ready, (i + 1) * KC + j + 1)
        act.wait_ge(N.parts_ready, i * KC + j + 1)
        nc.scalar.activation(N.h[0:r, j, :], psT[j][0:r, :], ACT.Identity, scale=mod[0:r, which + 1, j, b],
                             bias=mod[0:r, which, j, b]).then_inc(N.h_ready, 1)


def part_places(j):
    return ((HI + j, slice(0, P)), (LO + j, slice(0, P))) if j < FULL else ((STK, slice(0, STACK)), (STK, H_LO))


def norm_high(nc, act, N, hT, i):
    for j, (_, r) in enumerate(CHUNK):
        act.wait_ge(N.h_ready, (i + 1) * KC + j + 1)
        nc.scalar.activation(hT(*part_places(j)[0]), N.h[0:r, j, :], ACT.Copy).then_inc(N.hi_ready, 1)


def norm_low(nc, dve, N, hT, i):
    for j in range(KC):
        (hi, _), (lo, rows) = part_places(j)
        dve.wait_ge(N.hi_ready, i * KC + j + 1)
        nc.vector.tensor_tensor(hT(lo, rows), N.h[rows, j, :], hT(hi, rows).bitcast(F32), ALU.subtract
                                ).then_inc(N.parts_ready, 1)


def load_w_qkv(sp, T, W, sem):
    load_chunks(sp, lambda k: T.w_qkv[:, k, :], W.w_qkv, sem)


def split_weight(nc, eng, w, f32, whi, w_ready):
    for j, (_, r) in enumerate(CHUNK):
        hi, lo, part = (HI + j, LO + j, slice(0, P)) if j < FULL else (STK, STK, W_LO)
        nc.vector.tensor_copy(w[0:r, hi, :], f32[0:r, j, :]).then_inc(whi, 1)
        eng.wait_ge(whi, j + 1)
        nc.vector.tensor_tensor(w[part, lo, :], f32[part, j, :], w[part, hi, :].bitcast(F32), ALU.subtract
                                ).then_inc(w_ready, 1)


def over_blocks(eng, body):
    with eng.Fori(0, NBLK - 1) as i:
        body(i, True)
    body(NBLK - 1, False)


def entry(i):
    return slice(i // HALVES, i // HALVES + 1) if isinstance(i, int) else ds(i // HALVES, 1)


def qkv_stage(nc, T, l, W):
    with ExitStack() as ctx:
        sb, banks, sem = scopes(nc, ctx, f"qkv{l}")
        w = sb("wqkv_parts", [P, SLOT, 3 * C], F32R)
        bqk = sb("b_qk", [CHUNK_HEADS * D, QK_CHUNKS], F32)
        bv = sb("b_v", [P, C], F32)
        N = Norm(sb, sem)
        hT = sb("hT_parts", [P, SLOT, BLK], F32R)
        thirds = [sb(f"thirds{c}", [CHUNK_HEADS * D, 3, BLK], BF16) for c in range(QK_CHUNKS)]
        rest = [sb(f"rest{c}", [CHUNK_HEADS * D, BLK], F32) for c in range(QK_CHUNKS)]
        psT = banks("xT", KC)
        psQ = banks("qk", 2)
        psV = banks("v", 2)

        b_in = sem("b_in")
        whi_ready = sem("whi_ready")
        w_ready = sem("w_ready")
        v_filled = sem("v_filled")
        qk_ready = sem("qk_ready")
        v_ready = sem("v_ready")
        v_out = sem("v_out")
        first_ready = sem("first_ready")
        rest_ready = sem("rest_ready")
        second_ready = sem("second_ready")
        thirds_ready = sem("thirds_ready")
        stored = [sem(f"stored{c}") for c in range(QK_CHUNKS)]
        pieces = [len(chunk_pieces(c)) for c in range(QK_CHUNKS)]

        block = ctx.enter_context(nc.Block())

        @block.sync
        def _(sp):
            for c in range(QK_CHUNKS):
                r = chunk_rows(c)
                c0 = c * CHUNK_HEADS * D
                sp.dma_start(bqk[0:r, c:c + 1], W.b_qkv[c0:c0 + r].rearrange("(p o) -> p o", o=1)).then_inc(b_in, 16)
            sp.dma_start(bv[:], row(W.b_qkv[2 * C:3 * C], P)).then_inc(b_in, 16)
            with sp.Fori(0, B) as b:
                with sp.Fori(0, HALVES) as half:
                    i = b * HALVES + half
                    for c in range(QK_CHUNKS):
                        sp.wait_ge(thirds_ready, (i + 1) * QK_CHUNKS + c + 1)
                        for r0, r, qk, hg, off in chunk_pieces(c):
                            dst = T.qk_scr[ds(b * GPB + hg, 1), qk, :, off:off + r, ds(half * BLK, BLK)]
                            sp.dma_start(dst.rearrange("o t r n -> r (o t) n"), thirds[c][r0:r0 + r, :, :]
                                         ).then_inc(stored[c], 16)
            for c in range(QK_CHUNKS):
                sp.wait_ge(stored[c], 16 * pieces[c] * (NBLK + 1))

        @block.gpsimd
        def _(pool):
            v = T.V[:].rearrange("p g k (j d) -> p (g k j) d", j=HG)
            nc.gpsimd.memset(v[:, :, D:D + 1], 1.0).then_inc(v_filled, 1)
            nc.gpsimd.memset(v[:, :, D + 1:32], 0.0).then_inc(v_filled, 1)
            nc.gpsimd.memset(T.ones_rows[:], 1.0).then_inc(v_filled, 1)
            nc.gpsimd.memset(T.wp[:], 0.0).then_inc(v_filled, 1)
            pool.wait_ge(v_filled, 4)
            pool.sem_inc(thirds_ready, QK_CHUNKS)
            with pool.Fori(0, NBLK) as i:
                for c in range(QK_CHUNKS):
                    r = chunk_rows(c)
                    pool.wait_ge(second_ready, i * QK_CHUNKS + c + 1)
                    nc.gpsimd.tensor_tensor(thirds[c][0:r, 2, :], rest[c][0:r, :], thirds[c][0:r, 1, :],
                                            ALU.subtract).then_inc(thirds_ready, 1)

        @block.scalar
        def _(act):
            hT_at = lambda slot, rows: hT[rows, slot, :]
            act.sem_inc(N.h_ready, KC)
            for c in range(QK_CHUNKS):
                act.sem_inc(stored[c], 16 * pieces[c])
            norm_root(nc, act, N, 0)
            norm_modulate(nc, act, N, T.mod[l], 0, psT, entry(0), 0)
            norm_high(nc, act, N, hT_at, 0)
            act.wait_ge(b_in, 16 * (QK_CHUNKS + 1))

            def body(i, more):
                def second(c):
                    r = chunk_rows(c)
                    act.wait_ge(rest_ready, i * QK_CHUNKS + c + 1)
                    nc.scalar.activation(thirds[c][0:r, 1, :], rest[c][0:r, :], ACT.Identity
                                         ).then_inc(second_ready, 1)

                for c in range(QK_CHUNKS):
                    r = chunk_rows(c)
                    act.wait_ge(qk_ready, i * QK_CHUNKS + c + 1)
                    act.wait_ge(stored[c], (i + 1) * (16 * pieces[c]))
                    nc.scalar.activation(thirds[c][0:r, 0, :], psQ[c % 2][0:r, :], ACT.Identity,
                                         bias=bqk[0:r, c:c + 1]).then_inc(first_ready, 1)
                    if c:
                        second(c - 1)
                    if c == 1 and more:
                        norm_root(nc, act, N, i + 1)
                second(QK_CHUNKS - 1)
                if more:
                    norm_modulate(nc, act, N, T.mod[l], 0, psT, entry(i + 1), i + 1)
                    act.wait_ge(v_ready, (i + 1) * TPB)
                    norm_high(nc, act, N, hT_at, i + 1)

            over_blocks(act, body)

        @block.vector
        def _(dve):
            dve.sem_inc(v_out, 2)
            dve.sem_inc(N.parts_ready, KC)
            norm_variance(nc, dve, N, T.X, 0)
            norm_tiles(nc, dve, N, T.X, 0)
            split_weight(nc, dve, w, T.w_qkv, whi_ready, w_ready)
            dve.wait_ge(b_in, 16 * (QK_CHUNKS + 1))

            def body(i, more):
                norm_low(nc, dve, N, lambda slot, rows: hT[rows, slot, :], i)
                for c in range(QK_CHUNKS):
                    r = chunk_rows(c)
                    dve.wait_ge(first_ready, i * QK_CHUNKS + c + 1)
                    dve.wait_ge(thirds_ready, i * QK_CHUNKS + c + 1)
                    nc.vector.scalar_tensor_tensor(out=rest[c][0:r, :], in0=psQ[c % 2][0:r, :],
                                                   scalar=bqk[0:r, c:c + 1], in1=thirds[c][0:r, 0, :],
                                                   op0=ALU.add, op1=ALU.subtract
                                                   ).then_inc(rest_ready, 1)
                    if more and c == 0:
                        norm_variance(nc, dve, N, T.X, i + 1)
                    if more and c == 2:
                        norm_tiles(nc, dve, N, T.X, i + 1)
                b, half = (i // HALVES, i % HALVES)
                for t in range(TPB):
                    dve.wait_ge(v_ready, i * TPB + t + 1)
                    dst = T.V[:, ds(b * GPB, GPB), ds(half * TPB + t, 1), :].rearrange(
                        "p g o (j d) -> p (g o) j d", j=HG)[:, :, :, 0:D]
                    nc.vector.tensor_tensor(dst, psV[t % 2][:, 0:C].rearrange("p (g j d) -> p g j d", g=GPB, j=HG),
                                            bv[:].rearrange("p (g j d) -> p g j d", g=GPB, j=HG),
                                            ALU.add).then_inc(v_out, 1)

            over_blocks(dve, body)

        @block.tensor
        def _(pe):
            pe.sem_inc(N.xt_ready, KC)
            norm_transposes(nc, pe, N, T, psT, 0)
            pe.wait_ge(w_ready, KC)

            def body(i, more):
                for c in range(QK_CHUNKS):
                    r = chunk_rows(c)
                    c0 = c * CHUNK_HEADS * D
                    if c >= 2:
                        pe.wait_ge(rest_ready, i * QK_CHUNKS + c - 1)
                    for n, (ws, hs, rows) in enumerate(PASSES):
                        if c == 0 and n % len(PARTS) == 0:
                            pe.wait_ge(N.parts_ready, (i + 1) * KC + n // len(PARTS) + 1)
                        last = nc.tensor.matmul(psQ[c % 2][0:r, :], w[0:rows, ws, c0:c0 + r], hT[0:rows, hs, :],
                                                start=(n == 0), stop=(n == len(PASSES) - 1))
                    last.then_inc(qk_ready, 1)
                if more:
                    norm_transposes(nc, pe, N, T, psT, i + 1)
                for t in range(TPB):
                    pe.wait_ge(v_out, i * TPB + t + 1)
                    for n, (ws, hs, rows) in enumerate(PASSES):
                        last = nc.tensor.matmul(psV[t % 2][:, 0:C], hT[0:rows, hs, t * P:(t + 1) * P],
                                                w[0:rows, ws, 2 * C:3 * C], start=(n == 0), stop=(n == len(PASSES) - 1))
                    last.then_inc(v_ready, 1)
                pe.wait_ge(rest_ready, i * QK_CHUNKS + QK_CHUNKS)

            over_blocks(pe, body)


SLOTS = 3
assert HG * HALVES * KT % SLOTS == 1
STEPS = HALVES * KT
ITEMS = HG * KT * 2
PER_STEP = [5, 5, 5, 4, 5, 4, 5, 4, 5, 4, 5, 4, 5, 4, 0, 0]
COPY_STEP, RECIP_STEP, SPREAD_STEP, DIVIDE_STEP = KT + 1, KT + 3, KT + 5, KT + 6
MAX_FIRST = [sum(PER_STEP[:s]) for s in range(STEPS)]
UNIT = 2
TURN_STEP = STEPS - 2


def attention_stage(nc, T, l, W):
    with ExitStack() as ctx:
        sb, banks, sem = scopes(nc, ctx, f"att{l}")
        QS = [sb(f"QS{s}", [P, HG, SEQ], BF16) for s in range(SLOTS)]
        KS = [sb(f"KS{s}", [P, HG, SEQ], BF16) for s in range(SLOTS)]
        VG = [sb(f"VG{s}", [P, KT, HG * 32], F32) for s in range(SLOTS)]
        PR = [sb(f"probs{s}", [P, HG, BLK], F32) for s in range(2)]
        mx = sb("mx", [P, HG * KT, 2], F32)
        negm = sb("neg_max", [P, HG * KT], F32)
        mrow = sb("neg_max_rows", [HG * KT, 2, P], BF16)
        OZ = [sb(f"OZ{s}", [P, BLK], F32) for s in range(HALVES)]
        sums = [sb(f"sums{s}", [P, HG * BLK // P], F32) for s in range(HALVES)]
        inv = [sb(f"inverse{s}", [P, HG * BLK // P], F32) for s in range(HALVES)]
        RR = [sb(f"inverse_rows{s}", [P, BLK], F32) for s in range(HALVES)]
        psS = banks("scores", SLOTS)
        psM = banks("for_max", SLOTS)
        psO = banks("out", HALVES)

        ones_in = sem("ones_in")
        loaded = [sem(f"loaded{s}") for s in range(SLOTS)]
        m_loaded = [sem(f"m_loaded{s}") for s in range(SLOTS)]
        scores_ready = sem("scores_ready")
        exp_done = sem("exp_done")
        pv_done = sem("pv_done")
        row_ready = sem("row_ready")
        row_read = sem("row_read")
        negm_ready = sem("negm_ready")
        mT_ready = sem("mT_ready")
        mhi_ready = sem("mhi_ready")
        mrow_ready = sem("mrow_ready")
        oz_ready = sem("oz_ready")
        rows_zero = sem("rows_zero")
        sums_in = [sem(f"sums_in{s}") for s in range(HALVES)]
        inv_ready = [sem(f"inv_ready{s}") for s in range(HALVES)]
        inv_in = [sem(f"inv_in{s}") for s in range(HALVES)]
        z_ready = sem("z_ready")
        o_ready = sem("o_ready")
        wp_in = sem("wp_in")
        LOADS = 16 * (2 * len(Q_TERMS) + 1)

        def over_groups(eng, body):
            body(0, 0, 0)
            with eng.Fori(0, (GROUPS - 2) // SLOTS) as it:
                for n in range(1, SLOTS + 1):
                    body(it * SLOTS + n, n % SLOTS, it + n // SLOTS)
            body(GROUPS - 1, (GROUPS - 1) % SLOTS, (GROUPS - 1) // SLOTS)

        def score_bank(s, st, j):
            return psS[(s + st * HG + j) % SLOTS]

        def max_bank(s, m):
            return psM[(s + m) % SLOTS]

        def is_first(g):
            return isinstance(g, int) and g == 0

        def is_last(g):
            return isinstance(g, int) and g == GROUPS - 1

        def next_of(s, use):
            return (s + 1) % SLOTS, use + (s + 1) // SLOTS

        block = ctx.enter_context(nc.Block())

        @block.sync
        def _(sp):
            def load(g, s):
                for n, (q, k) in enumerate(zip(Q_TERMS, K_TERMS)):
                    for dst, which, term in ((QS[s], 0, q), (KS[s], 1, k)):
                        src = T.qk_scr[g:g + 1, which, term] if isinstance(g, int) else T.qk_scr[ds(g, 1), which, term]
                        sp.dma_start(dst[n * D:(n + 1) * D, :, :], src.rearrange("o (j d) n -> d (o j) n", j=HG)
                                     ).then_inc(loaded[s], 16)
                src = T.V[:, g] if isinstance(g, int) else T.V[:, ds(g, 1)].rearrange("p o k n -> p (o k) n")
                sp.dma_start(VG[s][:], src).then_inc(loaded[s], 16)

            def store_max(g, s):
                for e in range(2):
                    if e == 0:
                        sp.wait_ge(mhi_ready, g + 1)
                    else:
                        sp.wait_ge(mrow_ready, g + 2)
                    sp.dma_start(QS[s][ROWS + e:ROWS + e + 1, :, :], mrow[:, e, :]).then_inc(m_loaded[s], 16)

            def turn_sums(g, half):
                rows = slice(D, P, 32)
                sp.wait_ge(oz_ready, g * 2 + half + 1)
                sp.dma_start(sums[half][:], OZ[half][rows, :]).then_inc(sums_in[half], 16)
                if g == 0:
                    sp.wait_ge(rows_zero, HALVES)
                sp.wait_ge(inv_ready[half], g + 1)
                sp.dma_start(RR[half][rows, :], inv[half][:]).then_inc(inv_in[half], 16)

            for g in range(SLOTS):
                sp.dma_start(KS[g][ROWS:ROWS + 2, :, :], T.ones_rows[:]).then_inc(ones_in, 16)
                load(g, g)
            for j in range(HG):
                for g in range(GPB):
                    h = g * HG + j
                    sp.dma_start(T.wp[32 * j:32 * j + D, g, :], W.w_proj[h * D:(h + 1) * D, :]).then_inc(wp_in, 16)
            sp.dma_start(T.wp[D:D + 1, 0, :], row(W.b_proj, 1)).then_inc(wp_in, 16)
            store_max(0, 0)
            for g in range(GROUPS):
                if g and g - 1 + SLOTS < GROUPS:
                    sp.wait_ge(pv_done, g * STEPS + 2)
                    load(g - 1 + SLOTS, (g - 1) % SLOTS)
                if g:
                    turn_sums(g - 1, 1)
                turn_sums(g, 0)
                if g + 1 < GROUPS:
                    store_max(g + 1, (g + 1) % SLOTS)
            turn_sums(GROUPS - 1, 1)
            for half in range(HALVES):
                sp.wait_ge(inv_in[half], 16 * GROUPS)
            sp.wait_ge(wp_in, 16 * (H + 1))

        @block.gpsimd
        def _(pool):
            for half in range(HALVES):
                nc.gpsimd.memset(RR[half][:], 0.0).then_inc(rows_zero, 1)

        @block.scalar
        def _(act):
            act.sem_inc(exp_done, UNIT * SLOTS)

            def finish(g, half):
                act.wait_ge(pv_done, g * STEPS + (half + 1) * KT + 2)
                act.wait_ge(o_ready, g * 2 + half + 1)
                nc.scalar.activation(OZ[half][:], psO[half][:], ACT.Copy).then_inc(oz_ready, 1)

            def body(g, s, use):
                for st in range(STEPS):
                    act.wait_ge(pv_done, g * STEPS + st + 1)
                    for j in range(HG):
                        act.wait_ge(scores_ready, g * (HG * STEPS) + HG * st + j + 1)
                        nc.scalar.activation(PR[st % 2][:, j, :], score_bank(s, st, j)[:], ACT.Exp, scale=SCALE
                                             ).then_inc(exp_done, UNIT)
                    if st == COPY_STEP:
                        finish(g, 0)
                    if st == COPY_STEP - KT and not is_first(g):
                        finish(g - 1, 1)

            over_groups(act, body)
            finish(GROUPS - 1, 1)

        @block.vector
        def _(dve):
            dve.sem_inc(row_read, SLOTS)
            dve.sem_inc(mrow_ready, 1)
            dve.sem_inc(o_ready, 2)

            def reduce(g, s, m):
                dve.wait_ge(row_ready, g * ITEMS + m + 1)
                nc.vector.tensor_reduce(mx[:, m // 2, m % 2:m % 2 + 1], max_bank(s, m)[:], AX_X, ALU.max
                                        ).then_inc(row_read, 1)

            def combine(g):
                dve.wait_ge(row_read, (g + 1) * ITEMS + SLOTS)
                nc.vector.tensor_reduce(negm[:], mx[:], AX_X, ALU.max, negate=True).then_inc(negm_ready, 1)

            def rows_out(g, s, before):
                dve.wait_ge(mT_ready, g + 1)
                if before:
                    dve.wait_ge(m_loaded[before[0]], 32 * (before[1] + 1))
                nc.vector.tensor_copy(mrow[:, 0, :], max_bank(s, ITEMS)[0:HG * KT, 0:P]).then_inc(mhi_ready, 1)
                dve.wait_ge(mhi_ready, g + 1)
                nc.vector.tensor_tensor(mrow[:, 1, :], max_bank(s, ITEMS)[0:HG * KT, 0:P], mrow[:, 0, :], ALU.subtract
                                        ).then_inc(mrow_ready, 1)

            def recip(g, half):
                dve.wait_ge(sums_in[half], 16 * g + 16)
                nc.vector.reciprocal(inv[half][:], sums[half][:]).then_inc(inv_ready[half], 1)

            def divide(g, half):
                dve.wait_ge(z_ready, g * 2 + half + 1)
                dst = T.O[:, g] if isinstance(g, int) else T.O[:, ds(g, 1)].rearrange("p o n -> p (o n)")
                nc.vector.tensor_tensor(dst[:, half * BLK:(half + 1) * BLK], OZ[half][:], psO[half][:], ALU.mult
                                        ).then_inc(o_ready, 1)

            for m in range(ITEMS):
                reduce(0, 0, m)
            combine(0)
            rows_out(0, 0, None)

            def body(g, s, use):
                ns = next_of(s, use)[0]
                for st in range(STEPS):
                    if not is_last(g):
                        for m in range(MAX_FIRST[st], MAX_FIRST[st] + PER_STEP[st]):
                            reduce(g + 1, ns, m)
                        if st == TURN_STEP - 1:
                            combine(g + 1)
                        if st == TURN_STEP:
                            rows_out(g + 1, ns, (s, use))
                    for at, what in ((RECIP_STEP, recip), (DIVIDE_STEP, divide)):
                        if st == at - KT and not is_first(g):
                            what(g - 1, 1)
                        if st == at:
                            what(g, 0)

            over_groups(dve, body)
            recip(GROUPS - 1, 1)
            divide(GROUPS - 1, 1)

        @block.tensor
        def _(pe):
            pe.sem_inc(pv_done, 2)

            def max_item(g, s, m):
                j, t, half = m // (2 * KT), m // 2 % KT, m % 2
                pe.wait_ge(row_read, g * ITEMS + m + 1)
                nc.tensor.matmul(max_bank(s, m)[:], QS[s][0:ROWS, j, t * P:(t + 1) * P],
                                 KS[s][0:ROWS, j, half * BLK:(half + 1) * BLK], start=True, stop=True
                                 ).then_inc(row_ready, 1)

            def turn(g, s):
                pe.wait_ge(negm_ready, g + 1)
                nc.tensor.transpose(max_bank(s, ITEMS)[0:HG * KT, 0:P], negm[:], T.ident[:]).then_inc(mT_ready, 1)

            def scores(g, s, st, j):
                half, k = divmod(st, KT)
                pe.wait_ge(exp_done, g * (UNIT * HG * STEPS) + UNIT * (HG * st + j + 1))
                nc.tensor.matmul(score_bank(s, st, j)[:], KS[s][0:ROWS + 2, j, k * P:(k + 1) * P],
                                 QS[s][0:ROWS + 2, j, half * BLK:(half + 1) * BLK], start=True, stop=True
                                 ).then_inc(scores_ready, 1)

            def weigh(g, s, st, heads=range(HG)):
                half, k = divmod(st, KT)
                if k == 0 and 0 in heads:
                    pe.wait_ge(o_ready, g * 2 + half + 1)
                pe.wait_ge(exp_done, g * (UNIT * HG * STEPS) + UNIT * (HG * st + heads[-1] + 1 + SLOTS))
                for j in heads:
                    last = nc.tensor.matmul(psO[half][32 * j:32 * j + 32, :], VG[s][:, k, 32 * j:32 * j + 32],
                                            PR[st % 2][:, j, :], start=(k == 0), stop=(k == KT - 1),
                                            tile_position=(0, 32 * j))
                if heads[-1] == HG - 1:
                    last.then_inc(pv_done, 1)

            def spread(g, half):
                pe.wait_ge(inv_in[half], 16 * g + 16)
                nc.tensor.matmul(psO[half][:], T.sel[:], RR[half][:], start=True, stop=True).then_inc(z_ready, 1)

            pe.wait_ge(ones_in, 16 * SLOTS)
            pe.wait_ge(loaded[0], LOADS)
            for m in range(ITEMS):
                max_item(0, 0, m)
            turn(0, 0)

            def body(g, s, use):
                ns, nuse = next_of(s, use)
                pe.wait_ge(m_loaded[s], 32 * (use + 1))
                if not is_last(g):
                    pe.wait_ge(loaded[ns], LOADS * (nuse + 1))
                    pe.wait_ge(mrow_ready, g + 2)
                for st in range(STEPS):
                    items = [] if is_last(g) else list(range(MAX_FIRST[st], MAX_FIRST[st] + PER_STEP[st]))
                    last = (g, s, st - 1) if st else None if is_first(g) else (g - 1, (s - 1) % SLOTS, STEPS - 1)
                    fronts = [[lambda: scores(g, s, st, 0), lambda: scores(g, s, st, 1)],
                              [lambda: scores(g, s, st, 2)], [lambda: last and weigh(*last, range(0, 2))],
                              [lambda: scores(g, s, st, 3), lambda: last and weigh(*last, range(2, HG))]]
                    for n, front in enumerate(fronts):
                        for one in front:
                            one()
                        for m in items[n:n + 1]:
                            max_item(g + 1, ns, m)
                    if st == TURN_STEP and not is_last(g):
                        turn(g + 1, ns)
                    for m in items[len(fronts):]:
                        max_item(g + 1, ns, m)
                    if st == SPREAD_STEP - KT and not is_first(g):
                        spread(g - 1, 1)
                    if st == SPREAD_STEP:
                        spread(g, 0)

            over_groups(pe, body)
            weigh(GROUPS - 1, (GROUPS - 1) % SLOTS, STEPS - 1)
            spread(GROUPS - 1, 1)


class Staging:

    def __init__(self, sb, sem):
        self.w1, self.w2 = sb("w1_f32", [P, FF], F32), sb("w2_f32", [P, NF // KC, C], F32)
        self.w1_in, self.w2_in = sem("w1_in"), sem("w2_in")
        self.w1_split, self.w2_split = sem("w1_split"), sem("w2_split")
        self.hi_ready = sem("w_hi_ready")


def load_expert(sp, S, W, e, n):
    w2 = W.w2[e].rearrange("(f p) n -> p f n", p=P)
    for k in range(KC):
        if n * KC + k:
            sp.wait_ge(S.w1_split, n * KC + k + 1)
        if k < FULL:
            sp.dma_start(S.w1[:], W.w1[e, k * P:(k + 1) * P]).then_inc(S.w1_in, 16)
        else:
            for m in range(len(PARTS)):
                sp.dma_start(S.w1[m * REST:(m + 1) * REST], W.w1[e, FULL * P:C]).then_inc(S.w1_in, 16)
        if n * KC + k:
            sp.wait_ge(S.w2_split, n * KC + k + 1)
        sp.dma_start(S.w2[:], w2[:, 3 * k:3 * k + 3, :]).then_inc(S.w2_in, 16)


def load_biases(sp, W, e, b1, b2, sem):
    sp.dma_start(b1[:], W.b1[e].rearrange("(f p) -> p f", p=P), allow_slow_non_contiguous=True).then_inc(sem, 16)
    sp.dma_start(b2[:], row(W.b2[e], P)).then_inc(sem, 16)


def split_expert(nc, pool, S, w1, w2, n):
    for k, (_, r) in enumerate(CHUNK):
        hi, lo, part = (HI + k, LO + k, slice(0, P)) if k < FULL else (STK, STK, W_LO)
        pool.wait_ge(S.w1_in, 16 * (n * CHUNK_LOADS + (k + 1 if k < FULL else CHUNK_LOADS)))
        nc.gpsimd.tensor_copy(w1[0:r, hi, :], S.w1[0:r]).then_inc(S.hi_ready, 1)
        pool.wait_ge(S.hi_ready, n * 2 * KC + 2 * k + 1)
        nc.gpsimd.tensor_tensor(w1[part, lo, :], S.w1[part], w1[part, hi, :].bitcast(F32), ALU.subtract
                                ).then_inc(S.w1_split, 1)
        if k == FULL:
            pool.wait_ge(S.w1_split, (n + 1) * KC + 1)
        f = slice(3 * k, 3 * k + 3)
        pool.wait_ge(S.w2_in, 16 * (n * KC + k + 1))
        nc.gpsimd.tensor_copy(w2[:, 0, f, :], S.w2[:]).then_inc(S.hi_ready, 1)
        pool.wait_ge(S.hi_ready, n * 2 * KC + 2 * k + 2)
        nc.gpsimd.tensor_tensor(w2[:, 1, f, :], S.w2[:], w2[:, 0, f, :].bitcast(F32), ALU.subtract
                                ).then_inc(S.w2_split, 1)


def project_stage(nc, T, l, W, moe):
    with ExitStack() as ctx:
        sb, banks, sem = scopes(nc, ctx, f"proj{l}")
        upd = sb("update", [P, TPB, C], F32)
        N = Norm(sb, sem)
        S = Staging(sb, sem)
        psT = banks("xT", KC)
        psP = banks("proj", TPB)
        psL = banks("logits", 1)[0]
        psLT = psL[:, 0:TPB * E]

        proj_ready = sem("proj_ready")
        gated = sem("gated")
        added = sem("added")
        bias_in = sem("bias_in")
        wg_in = sem("wg_in")
        wg_zero = sem("wg_zero")
        wghi_ready = sem("wghi_ready")
        wg_ready = sem("wg_ready")
        lg_ready = sem("lg_ready")
        lg_copied = sem("lg_copied")
        lgT_ready = sem("lgT_ready")
        lgT_read = sem("lgT_read")
        chain = sem("route_steps")
        ex_ready = sem("ex_ready")
        if moe:
            wgs = sb("w_gate_f32", [P, KC, P], F32)
            wg = sb("w_gate_parts", [P, SLOT, P], F32R)
            lg = sb("logits_sb", [E, BLK], F32)
            LG = sb("logits_all", [P, TILES, E], F32)
            rank = sb("rank", [P, TILES, E], F32)
            cmp = sb("cmp", [P, TILES], F32)
            top = sb("top", [P, TILES], F32)
            ex = sb("ex", [P, TILES, E], F32)
            den = sb("den", [P, TILES], F32)

        def over_inner_blocks(eng, body):
            body(0, False, True)
            with eng.Fori(1, NBLK - 1) as i:
                body(i, True, True)
            body(NBLK - 1, True, False)

        block = ctx.enter_context(nc.Block())

        @block.sync
        def _(sp):
            if moe:
                sp.wait_ge(wg_zero, 1)
                load_chunks(sp, lambda k: wgs[:, k, 0:E], W.w_gate, wg_in)
            load_expert(sp, S, W, 0, 0)
            load_biases(sp, W, 0, T.b1[0], T.b2[0], bias_in)
            sp.wait_ge(bias_in, 32)

        @block.gpsimd
        def _(pool):
            if moe:
                nc.gpsimd.memset(wgs[:], 0.0).then_inc(wg_zero, 1)
            pool.sem_inc(S.w1_split, 1)
            pool.sem_inc(S.w2_split, 1)
            split_expert(nc, pool, S, T.w1[0], T.w2[0], 0)

        @block.scalar
        def _(act):
            act.sem_inc(N.h_ready, KC)
            norm_root(nc, act, N, 0)

            def copy_logits(i):
                act.wait_ge(lg_ready, i + 1)
                nc.scalar.activation(lg[:], psL[0:E, :], ACT.Copy).then_inc(lg_copied, 1)

            def body(i, before, more):
                if more:
                    norm_root(nc, act, N, i + 1)
                if moe and before:
                    copy_logits(i - 1)
                norm_modulate(nc, act, N, T.mod[l], 2, psT, entry(i), i)
                norm_high(nc, act, N, lambda slot, rows: T.hT[rows, slot, ds(i * BLK, BLK)], i)

            over_inner_blocks(act, body)
            if moe:
                copy_logits(NBLK - 1)
                act.wait_ge(chain, 2)
                nc.scalar.activation(ex[:], ex[:], ACT.Exp).then_inc(ex_ready, 1)

        @block.vector
        def _(dve):
            dve.sem_inc(N.parts_ready, KC)

            def update(i):
                for t in range(TPB):
                    dve.wait_ge(proj_ready, i * TPB + t + 1)
                    nc.vector.tensor_tensor(upd[:, t, :], psP[t][:, 0:C],
                                            T.gate[l][:, 0, entry(i), :].rearrange("p o c -> p (o c)"), ALU.mult
                                            ).then_inc(gated, 1)
                dve.wait_ge(gated, i * TPB + TPB)
                x = T.X[:, ds(i * TPB, TPB), :]
                nc.vector.tensor_tensor(x, x, upd[:], ALU.add).then_inc(added, 1)
                wait_alone(dve, added, i + 1, N.passed)
                norm_variance(nc, dve, N, T.X, i)
                norm_tiles(nc, dve, N, T.X, i)

            def copy_logits(i):
                dve.wait_ge(lgT_ready, i + 1)
                nc.vector.tensor_copy(LG[:, ds(i * TPB, TPB), :], psLT.rearrange("p (t e) -> p t e", e=E)
                                      ).then_inc(lgT_read, 1)

            update(0)
            if moe:
                dve.wait_ge(wg_in, 16 * CHUNK_LOADS)
                split_weight(nc, dve, wg, wgs, wghi_ready, wg_ready)

            def body(i, before, more):
                if more:
                    update(i + 1)
                norm_low(nc, dve, N, lambda slot, rows: T.hT[rows, slot, ds(i * BLK, BLK)], i)
                if moe and before:
                    copy_logits(i - 1)

            over_inner_blocks(dve, body)
            if not moe:
                return
            copy_logits(NBLK - 1)
            dve.wait_ge(lgT_read, NBLK)
            n = 0

            def step(ins):
                nonlocal n
                n += 1
                ins.then_inc(chain, 1)
                dve.wait_ge(chain, n)

            step(nc.vector.tensor_reduce(top[:], LG[:], AX_X, ALU.max))
            step(nc.vector.tensor_tensor(ex[:], LG[:], top[:].rearrange("p (t o) -> p t o", o=1).broadcast_to([P, TILES, E]),
                                         ALU.subtract))
            step(nc.vector.memset(rank[:], 0.0))
            for a in range(E):
                for c in range(a + 1, E):
                    step(nc.vector.tensor_tensor(cmp[:], LG[:, :, a], LG[:, :, c], ALU.is_ge))
                    step(nc.vector.tensor_tensor(rank[:, :, c], rank[:, :, c], cmp[:], ALU.add))
                    step(nc.vector.scalar_tensor_tensor(out=rank[:, :, a], in0=rank[:, :, a], scalar=1.0, in1=cmp[:],
                                                        op0=ALU.add, op1=ALU.subtract))
            step(nc.vector.tensor_scalar(rank[:], rank[:], 2.0, None, ALU.is_lt))
            dve.wait_ge(ex_ready, 1)
            step(nc.vector.tensor_tensor(ex[:], ex[:], rank[:], ALU.mult))
            step(nc.vector.reduce_sum(den[:], ex[:], AX_X))
            step(nc.vector.reciprocal(den[:], den[:]))
            step(nc.vector.tensor_tensor(T.cw[:], ex[:], den[:].rearrange("p (t o) -> p t o", o=1).broadcast_to([P, TILES, E]),
                                         ALU.mult))

        @block.tensor
        def _(pe):
            pe.sem_inc(N.xt_ready, KC)

            def project(i):
                b, half = divmod(i, HALVES)
                for t in range(TPB):
                    if i:
                        pe.wait_ge(gated, (i - 1) * TPB + t + 1)
                    at = half * BLK + t * P
                    for g in range(GPB):
                        last = nc.tensor.matmul(psP[t][:, 0:C], T.O[:, b * GPB + g, at:at + P], T.wp[:, g, :],
                                                start=(g == 0), stop=(g == GPB - 1))
                    last.then_inc(proj_ready, 1)

            def logits(i):
                pe.wait_ge(N.parts_ready, (i + 2) * KC)
                if i == 0:
                    pe.wait_ge(wg_ready, KC)
                else:
                    pe.wait_ge(lgT_read, i)
                for n, (ws, hs, rows) in enumerate(PASSES):
                    last = nc.tensor.matmul(psL[:], wg[0:rows, ws, :], T.hT[0:rows, hs, i * BLK:(i + 1) * BLK],
                                            start=(n == 0), stop=(n == len(PASSES) - 1))
                last.then_inc(lg_ready, 1)

            def turn_logits(i):
                pe.wait_ge(lg_copied, i + 1)
                for t in range(TPB):
                    last = nc.tensor.transpose(psLT[:, t * E:(t + 1) * E], lg[:, t * P:(t + 1) * P], T.ident[0:E, 0:E])
                last.then_inc(lgT_ready, 1)

            project(0)
            for i in range(NBLK):
                if i + 1 < NBLK:
                    project(i + 1)
                if moe and i:
                    logits(i - 1)
                norm_transposes(nc, pe, N, T, psT, i)
                if moe and i:
                    turn_logits(i - 1)
            if moe:
                logits(NBLK - 1)
                turn_logits(NBLK - 1)


def mlp_stage(nc, T, l, W, experts, following=None, out=None):
    with ExitStack() as ctx:
        sb, banks, sem = scopes(nc, ctx, f"mlp{l}")
        SETS = min(2, experts)
        RING = 3
        LAG = 2
        w1, w2, b1, b2 = T.w1, T.w2, T.b1, T.b2
        taken = 0

        def in_O(name, shape, dt):
            nonlocal taken
            n = shape[1] * (shape[2] if len(shape) == 3 else 1)
            ap = T.O[:].rearrange("p g n -> p (g n)")[:, taken:taken + n]
            taken += n
            return ap if len(shape) == 2 else ap.rearrange("p (a b) -> p a b", a=shape[1])

        if experts > 1:
            S = Staging(in_O, sem)
            w1 = [w1[0], sb("w1_parts1", [P, SLOT, FF], F32R)]
            w2 = [w2[0], sb("w2_parts1", [P, 2, NF, C], F32R)]
            b1 = [b1[0], sb("b1_1", [P, NF], F32)]
            b2 = [b2[0], sb("b2_1", [P, C], F32)]
        g32 = [in_O(f"gelu{n}", [P, BLK], F32) for n in range(RING)]
        upd = in_O("update", [P, TPB, C], F32)
        gb2 = in_O("gated_b2", [P, C], F32)
        hp = [sb(f"hidden_parts{n}", [P, 2, BLK], F32R) for n in range(RING)]
        psH = banks("hidden", RING)
        psY = banks("y", TPB)

        passed = sem("waits_passed")
        bias_in = [sem(f"bias_in{s}") for s in range(SETS)]
        bias_used = sem("bias_used")
        h_ready = sem("h_ready")
        gelu_ready = sem("gelu_ready")
        hi_ready = sem("hi_ready")
        parts_ready = sem("parts_ready")
        used = sem("hidden_used")
        y_read = sem("y_read")
        steps = sem("update_steps")
        stored = sem("stored")
        next_in = sem("next_in")

        def over_experts(eng, body):
            if experts == 1:
                body(0, 0, 0)
            else:
                with eng.Fori(0, experts // SETS) as it:
                    for s in range(SETS):
                        body(it * SETS + s, s, it)

        block = ctx.enter_context(nc.Block())

        @block.sync
        def _(sp):
            if following is not None:
                load_w_qkv(sp, T, following, next_in)
                sp.wait_ge(next_in, 16 * CHUNK_LOADS)
            if experts > 1:
                sp.sem_inc(bias_in[0], 32)
            for e in range(1, experts):
                load_expert(sp, S, W, e, e - 1)
                if e >= SETS:
                    sp.wait_ge(bias_used, e - SETS + 1)
                load_biases(sp, W, e, b1[e % SETS], b2[e % SETS], bias_in[e % SETS])
            if out is not None:
                rows = out.rearrange("b (t p) c -> p (b t) c", p=P)
                for i in range(NBLK):
                    sp.wait_ge(steps, ((experts - 1) * NBLK + i) * 3 + 3)
                    sp.dma_start(rows[:, i * TPB:(i + 1) * TPB], T.X[:, i * TPB:(i + 1) * TPB]).then_inc(stored, 16)
                sp.wait_ge(stored, 16 * NBLK)

        @block.gpsimd
        def _(pool):
            if experts > 1:
                pool.sem_inc(S.w1_split, 1)
                pool.sem_inc(S.w2_split, 1)
            for e in range(1, experts):
                if e >= SETS:
                    pool.wait_ge(used, (e - SETS + 1) * NBLK * NF + RING)
                split_expert(nc, pool, S, w1[e % SETS], w2[e % SETS], e - 1)

        @block.scalar
        def _(act):
            def body(e, s, use):
                if experts > 1:
                    act.wait_ge(bias_in[s], (use + 1) * 32)
                with act.Fori(0, NBLK) as i:
                    at = (e * NBLK + i) * NF
                    for f in range(NF):
                        act.wait_ge(h_ready, at + f + 1)
                        act.wait_ge(parts_ready, at + f + 1)
                        nc.scalar.activation(g32[f % RING][:], psH[f % RING][:], ACT.Gelu_apprx_tanh,
                                             bias=b1[s][:, f:f + 1]).then_inc(gelu_ready, 1)

            over_experts(act, body)

        @block.vector
        def _(dve):
            dve.sem_inc(parts_ready, RING)
            dve.sem_inc(y_read, TPB)

            def body(e, s, use):
                if experts > 1:
                    wait_alone(dve, bias_in[s], (use + 1) * 32, passed)
                with dve.Fori(0, NBLK) as i:
                    n = e * NBLK + i
                    gate = T.gate[l][:, 1, entry(i), :].rearrange("p o c -> p (o c)")

                    def weight(t):
                        return 1.0 if experts == 1 else \
                            T.cw[:, ds(i * TPB + t, 1), ds(e, 1)].rearrange("p t e -> p (t e)")

                    for f in range(NF):
                        dve.wait_ge(gelu_ready, n * NF + f + 1)
                        dve.wait_ge(used, n * NF + f + 1)
                        nc.vector.tensor_copy(hp[f % RING][:, 0, :], g32[f % RING][:]).then_inc(hi_ready, 1)
                        dve.wait_ge(hi_ready, n * NF + f + 1)
                        nc.vector.tensor_tensor(hp[f % RING][:, 1, :], g32[f % RING][:],
                                                hp[f % RING][:, 0, :].bitcast(F32), ALU.subtract
                                                ).then_inc(parts_ready, 1)
                        if f == NF // 2:
                            nc.vector.tensor_tensor(gb2[:], gate, b2[s][:], ALU.mult).then_inc(steps, 1)
                            dve.wait_ge(steps, n * 3 + 1)
                            for t in range(TPB):
                                x = T.X[:, ds(i * TPB + t, 1), :].rearrange("p o c -> p (o c)")
                                last = nc.vector.scalar_tensor_tensor(out=x, in0=gb2[:], scalar=weight(t), in1=x,
                                                                      op0=ALU.mult, op1=ALU.add)
                            last.then_inc(steps, 1)
                    dve.wait_ge(used, n * NF + NF + RING)
                    for t in range(TPB):
                        nc.vector.scalar_tensor_tensor(out=upd[:, t, :], in0=psY[t][:, 0:C], scalar=weight(t), in1=gate,
                                                       op0=ALU.mult, op1=ALU.mult).then_inc(y_read, 1)
                    dve.wait_ge(y_read, n * TPB + 2 * TPB)
                    dve.wait_ge(steps, n * 3 + 2)
                    x = T.X[:, ds(i * TPB, TPB), :]
                    nc.vector.tensor_tensor(x, x, upd[:], ALU.add).then_inc(steps, 1)
                dve.sem_inc(bias_used, 1)

            over_experts(dve, body)

        @block.tensor
        def _(pe):
            pe.sem_inc(used, RING)

            def body(e, s, use):
                if experts > 1:
                    pe.wait_ge(S.w1_split, e * KC + 1)
                    wait_alone(pe, S.w2_split, e * KC + 1, passed)
                with pe.Fori(0, NBLK) as i:
                    blk = e * NBLK + i

                    def up(f):
                        pe.wait_ge(parts_ready, blk * NF + f + 1)
                        for n, (ws, hs, rows) in enumerate(PASSES):
                            last = nc.tensor.matmul(psH[f % RING][:], w1[s][0:rows, ws, f * P:(f + 1) * P],
                                                    T.hT[0:rows, hs, ds(i * BLK, BLK)],
                                                    start=(n == 0), stop=(n == len(PASSES) - 1))
                        last.then_inc(h_ready, 1)

                    def down(f):
                        pe.wait_ge(parts_ready, blk * NF + f + 1 + RING)
                        for t in range(TPB):
                            if f == 0:
                                pe.wait_ge(y_read, blk * TPB + t + 1)
                            for n, (wpart, hpart) in enumerate(PARTS):
                                last = nc.tensor.matmul(psY[t][:, 0:C], hp[f % RING][:, hpart, t * P:(t + 1) * P],
                                                        w2[s][:, wpart, f, :], start=(f == 0 and n == 0),
                                                        stop=(f == NF - 1 and n == 2))
                        last.then_inc(used, 1)

                    for f in range(NF):
                        up(f)
                        if f >= LAG:
                            down(f - LAG)
                    for f in range(NF - LAG, NF):
                        down(f)

            over_experts(pe, body)


class Shared:
    pass


class Layer:

    def __init__(self, A, prefix, w_ada, b_ada, w_qkv, w_proj, w1, b1, w2, b2):
        self.w_ada, self.b_ada = A[prefix + w_ada], A[prefix + b_ada]
        self.w_qkv, self.b_qkv = A[prefix + w_qkv], A[prefix + "b_qkv"]
        self.w_proj, self.b_proj = A[prefix + w_proj], A[prefix + "b_proj"]
        self.w1, self.b1, self.w2, self.b2 = (A[prefix + n] for n in (w1, b1, w2, b2))
        if len(self.w1.shape) == 2:
            self.w1 = self.w1.rearrange("(o c) n -> o c n", o=1)
            self.b1 = self.b1.rearrange("(o c) -> o c", o=1)
            self.w2 = self.w2.rearrange("(o c) n -> o c n", o=1)
            self.b2 = self.b2.rearrange("(o c) -> o c", o=1)


def program(nc, A, out):
    layers = [Layer(A, "L0_cond_", "W_ada", "b_ada", "W_qkv", "W_proj", "W_fc1", "b_fc1", "W_fc2", "b_fc2"),
              Layer(A, "L1_cond_", "w_adaln", "b_adaln", "w_qkv", "w_proj", "w1", "b1", "w2", "b2")]
    layers[1].w_gate = A["L1_cond_w_gate"]
    with ExitStack() as ctx:
        sb = lambda name, shape, dt: ctx.enter_context(nc.sbuf_tensor(name, shape, dt))
        T = Shared()
        T.X = sb("X", [P, TILES, C], F32)
        T.ident = sb("ident", [P, P], F32)
        T.mod = [sb(f"mod{l}", [P, 4, KC, B], F32) for l in range(2)]
        T.gate = [sb(f"gate{l}", [P, 2, B, C], F32) for l in range(2)]
        T.cw = sb("expert_weights", [P, TILES, E], F32)
        T.sel = sb("sel", [P, P], F32)
        T.qk_scr = nc.dram_tensor("qk_thirds", (GROUPS, 2, 3, HG * D, SEQ), BF16).ap()
        T.O = sb("heads_out", [P, GROUPS, SEQ], F32)
        T.w_qkv = T.O[:].rearrange("p g n -> p (g n)")[:, GROUPS * SEQ - KC * 3 * C:].rearrange("p (k n) -> p k n", k=KC)
        T.wp = sb("w_proj", [P, GPB, C], F32)
        modulation(nc, T, A["x"], A["cond_1152"], layers)
        for l, W in enumerate(layers):
            own = lambda scope, name, shape, dt: scope.enter_context(nc.sbuf_tensor(f"{name}{l}", shape, dt))
            with ExitStack() as scope:
                T.V = own(scope, "V", [P, GROUPS, KT, HG * 32], F32)
                T.ones_rows = own(scope, "ones_rows", [2, HG, SEQ], BF16)
                qkv_stage(nc, T, l, W)
                attention_stage(nc, T, l, W)
            with ExitStack() as scope:
                T.hT = own(scope, "hT", [P, SLOT, TOKENS], F32R)
                T.w1 = [own(scope, "w1_parts", [P, SLOT, FF], F32R)]
                T.w2 = [own(scope, "w2_parts", [P, 2, NF, C], F32R)]
                T.b1 = [own(scope, "b1", [P, NF], F32)]
                T.b2 = [own(scope, "b2", [P, C], F32)]
                project_stage(nc, T, l, W, moe=(l == 1))
                if l == 0:
                    mlp_stage(nc, T, l, W, 1, following=layers[1])
                else:
                    mlp_stage(nc, T, l, W, E, out=out)


_INS = ['x', 'cond_1152', 'L0_cond_W_qkv', 'L0_cond_b_qkv', 'L0_cond_W_proj', 'L0_cond_b_proj', 'L0_cond_W_fc1',
        'L0_cond_b_fc1', 'L0_cond_W_fc2', 'L0_cond_b_fc2', 'L0_cond_W_ada', 'L0_cond_b_ada', 'L1_cond_w_adaln',
        'L1_cond_b_adaln', 'L1_cond_w_qkv', 'L1_cond_b_qkv', 'L1_cond_w_proj', 'L1_cond_b_proj', 'L1_cond_w_gate',
        'L1_cond_w1', 'L1_cond_b1', 'L1_cond_w2', 'L1_cond_b2']


def kernel(**inputs):
    import numpy as _np
    import concourse.bacc as _bacc
    from concourse import mybir as _mybir
    from concourse.bass_utils import run_bass_kernel_spmd as _run

    nc = _bacc.Bacc("TRN2", target_bir_lowering=False, num_devices=1)
    arrays, args = {}, {}
    for name in _INS:
        a = _np.ascontiguousarray(inputs[name])
        arrays[f"in_{name}_dram"] = a
        args[name] = nc.dram_tensor(f"in_{name}_dram", a.shape, _mybir.dt.from_np(a.dtype), kind="ExternalInput").ap()
    out = nc.dram_tensor("out_0_dram", (B, SEQ, C), F32, kind="ExternalOutput").ap()
    program(nc, args, out)
    r = _run(nc, [arrays], core_ids=[0])
    return r.results[0]["out_0_dram"]
```

```python
from contextlib import ExitStack

import concourse.bass as bass
from concourse import mybir

ACT = mybir.ActivationFunctionType
ALU = mybir.AluOpType
AX_X = mybir.AxisListType.X
F32 = mybir.dt.float32
F32R = mybir.dt.float32r
BF16 = mybir.dt.bfloat16
ds = bass.ds

P = 128
B, SEQ, C, H = 2, 1024, 288, 16
D = C // H
FF = 4 * C
E = 4
TOKENS = B * SEQ
TILES = TOKENS // P
FULL = C // P
REST = C - FULL * P
KC = FULL + 1
NF = FF // P
BLK = 512
TPB = BLK // P
NBLK = TOKENS // BLK
HALVES = SEQ // BLK
EPS = 1e-6
SCALE = float(D) ** -0.5
HG = 4
GPB = H // HG
GROUPS = B * GPB
KT = SEQ // P
PARTS = ((0, 0), (1, 0), (0, 1))
STACK = len(PARTS) * REST
W_LO = slice(REST, 2 * REST)
H_LO = slice(2 * REST, STACK)
HI, LO, STK = 0, FULL, 2 * FULL
SLOT = 2 * FULL + 1
PASSES = [(k + FULL * wp, k + FULL * hp, P) for k in range(FULL) for wp, hp in PARTS] + [(STK, STK, STACK)]
CX = C + STACK - REST
CHUNK = [(0, P), (P, P), (2 * P, STACK)]
Q_TERMS, K_TERMS = (0, 0, 0, 1, 1, 2), (0, 1, 2, 0, 1, 0)
ROWS = len(Q_TERMS) * D
QK_HEADS = 2 * H
CHUNK_HEADS = P // D
QK_CHUNKS = -(-QK_HEADS // CHUNK_HEADS)


def chunk_rows(c):
    return min(CHUNK_HEADS, QK_HEADS - CHUNK_HEADS * c) * D


def chunk_pieces(c):
    heads = range(CHUNK_HEADS * c, min(CHUNK_HEADS * (c + 1), QK_HEADS))
    out = []
    for n in sorted({h // HG for h in heads}):
        own = [h for h in heads if h // HG == n]
        out.append(((own[0] - heads[0]) * D, len(own) * D, n // GPB, n % GPB, own[0] % HG * D))
    return out


def load_chunks(eng, dst, src, sem):
    for k in range(FULL):
        eng.dma_start(dst(k)[:], src[k * P:(k + 1) * P]).then_inc(sem, 16)
    for n in range(len(PARTS)):
        eng.dma_start(dst(FULL)[n * REST:(n + 1) * REST], src[FULL * P:C]).then_inc(sem, 16)


CHUNK_LOADS = FULL + len(PARTS)


def row(ap, n):
    return ap.rearrange("(o c) -> o c", o=1).broadcast_to([n, ap.shape[0]])


def scopes(nc, ctx, stage):
    def sb(name, shape, dt):
        return ctx.enter_context(nc.sbuf_tensor(f"{stage}_{name}", shape, dt))

    def banks(name, n, width=1):
        shape = [P, 512] if width == 1 else [P, width, 512]
        return [ctx.enter_context(nc.psum_tensor(f"{stage}_{name}{i}", shape, F32)) for i in range(n)]

    sems = []

    @ctx.callback
    def _():
        nc.clear_and_free_semaphores(sems)
        nc.all_engine_barrier()

    def sem(name):
        sems.append(nc.alloc_semaphore(name=f"{stage}_{name}"))
        return sems[-1]

    return sb, banks, sem


def modulation(nc, T, x, cond, layers):
    with ExitStack() as ctx:
        sb, banks, sem = scopes(nc, ctx, "ada")
        CK = C // 3
        NK = C // CK
        NA = P // 32
        AW = 6 * C // NA
        cT = sb("cT", [CK, NK, B], F32)
        sc = sb("sc", [CK, NK, B], F32)
        ones = sb("ones", [B, P], F32)
        pick = sb("pick_entry", [B, B, P], F32)
        w = [sb(f"w_ada{l}", [CK, NK, 6 * C], F32) for l in range(2)]
        brow = [sb(f"b_ada_rows{l}", [B, 6 * C], F32) for l in range(2)]
        arow = [sb(f"ada_rows{l}", [B, 6 * C], F32) for l in range(2)]
        acols = [sb(f"ada_cols{l}", [B, 4, CX], F32) for l in range(2)]
        ps = banks("ada", 2)
        psT = banks("adaT", 1)[0]
        psG = banks("gateP", 2 * B)

        cond_in = sem("cond_in")
        b_in = sem("b_in")
        w_in = [sem(f"w_in{l}") for l in range(2)]
        x_in = sem("x_in")
        ident0 = sem("ident0")
        ident_ready = sem("ident_ready")
        ones_ready = sem("ones_ready")
        silu_ready = sem("silu_ready")
        pick_ready = sem("pick_ready")
        sel_zero = sem("sel_zero")
        sel_ready = sem("sel_ready")
        rows_ready = sem("rows_ready")
        rows_out = sem("rows_out")
        acols_ready = sem("acols_ready")
        cols_ready = sem("cols_ready")
        cols_out = sem("cols_out")
        gate_ready = sem("gate_ready")
        gate_out = sem("gate_out")

        block = ctx.enter_context(nc.Block())

        @block.sync
        def _(sp):
            for b in range(B):
                for j in range(NK):
                    sp.dma_start(cT[:, j, b:b + 1], cond[b, j * CK:(j + 1) * CK].rearrange("(p o) -> p o", o=1)
                                 ).then_inc(cond_in, 16)
            for l in range(2):
                sp.dma_start(brow[l][:], row(layers[l].b_ada, B)).then_inc(b_in, 16)
            for l in range(2):
                sp.dma_start(w[l][:], layers[l].w_ada.rearrange("(k p) n -> p k n", p=CK)).then_inc(w_in[l], 16)
            sp.dma_start(T.X[:], x.rearrange("b (t p) c -> p (b t) c", p=P)).then_inc(x_in, 16)
            load_w_qkv(sp, T, layers[0], x_in)
            sp.wait_ge(x_in, 16 * (1 + CHUNK_LOADS))

        @block.gpsimd
        def _(pool):
            nc.gpsimd.memset(T.ident[:], 0.0).then_inc(ident0, 1)
            pool.wait_ge(ident0, 1)
            nc.gpsimd.affine_select(out=T.ident[:], in_=T.ident[:], compare_op=ALU.not_equal, fill=1.0, base=0,
                                    pattern=[[-1, P]], channel_multiplier=1).then_inc(ident_ready, 1)
            nc.gpsimd.memset(T.sel[:], 0.0).then_inc(sel_zero, 1)
            pool.wait_ge(sel_zero, 1)
            v = T.sel[:].rearrange("p (j d) -> p j d", j=HG)
            nc.gpsimd.affine_select(out=v, in_=v, compare_op=ALU.not_equal, fill=1.0, base=-D,
                                    pattern=[[-32, HG], [0, 32]], channel_multiplier=1).then_inc(sel_ready, 1)
            pool.wait_ge(sel_ready, 1)

        @block.scalar
        def _(act):
            act.wait_ge(cond_in, 16 * B * NK)
            nc.scalar.activation(sc[:], cT[:], ACT.Silu).then_inc(silu_ready, 1)

        @block.vector
        def _(dve):
            nc.vector.memset(ones[:], 1.0).then_inc(ones_ready, 1)
            dve.wait_ge(ones_ready, 1)
            dve.wait_ge(ident_ready, 1)
            for b in range(B):
                last = nc.vector.tensor_scalar(pick[:, b, :], ones[:], T.ident[0:B, b:b + 1], None, ALU.mult)
            last.then_inc(pick_ready, 1)
            dve.wait_ge(b_in, 32)
            for l in range(2):
                dve.wait_ge(rows_ready, l + 1)
                for n in range(NA):
                    last = nc.vector.tensor_tensor(arow[l][:, n * AW:(n + 1) * AW], ps[l][32 * n:32 * n + B, 0:AW],
                                                   brow[l][:, n * AW:(n + 1) * AW], ALU.add)
                last.then_inc(rows_out, 1)
                dve.wait_ge(rows_out, l + 1)
                for n, part in enumerate((0, 1, 3, 4)):
                    c0 = part * C
                    nc.vector.tensor_scalar(acols[l][:, n, 0:FULL * P], arow[l][:, c0:c0 + FULL * P],
                                            float(n % 2), None, ALU.add)
                    tail = arow[l][:, c0 + FULL * P:c0 + C].rearrange("p (o c) -> p o c", o=1)
                    last = nc.vector.tensor_scalar(acols[l][:, n, FULL * P:CX].rearrange("p (o c) -> p o c", c=REST),
                                                   tail.broadcast_to([B, len(PARTS), REST]), float(n % 2), None, ALU.add)
                last.then_inc(acols_ready, 1)
                for g in range(2):
                    for b in range(B):
                        n = 2 * g + b
                        dve.wait_ge(gate_ready, 2 * B * l + n + 1)
                        nc.vector.tensor_copy(T.gate[l][:, g, b, :], psG[n][:, 0:C]).then_inc(gate_out, 1)
                dve.wait_ge(cols_ready, l + 1)
                for j, (_, r) in enumerate(CHUNK):
                    last = nc.vector.tensor_copy(T.mod[l][0:r, :, j], psT[0:r, j * 4 * B:(j + 1) * 4 * B].rearrange(
                        "p (n b) -> p n b", n=4))
                last.then_inc(cols_out, 1)

        @block.tensor
        def _(pe):
            pe.wait_ge(silu_ready, 1)

            def rows(l):
                pe.wait_ge(w_in[l], 16)
                for j in range(NK):
                    for n in range(NA):
                        last = nc.tensor.matmul(ps[l][32 * n:32 * n + B, 0:AW], sc[:, j, :], w[l][:, j, n * AW:(n + 1) * AW],
                                                start=(j == 0), stop=(j == NK - 1), tile_position=(0, 32 * n))
                last.then_inc(rows_ready, 1)

            for l in range(2):
                rows(l)
                pe.wait_ge(pick_ready, 1)
                pe.wait_ge(rows_out, l + 1)
                for g, part in enumerate((2, 5)):
                    for b in range(B):
                        n = 2 * g + b
                        if l:
                            pe.wait_ge(gate_out, n + 1)
                        nc.tensor.matmul(psG[n][:, 0:C], pick[:, b, :], arow[l][:, part * C:(part + 1) * C],
                                         start=True, stop=True).then_inc(gate_ready, 1)
                pe.wait_ge(acols_ready, l + 1)
                if l:
                    pe.wait_ge(cols_out, 1)
                for n in range(4):
                    for j, (c0, r) in enumerate(CHUNK):
                        at = (j * 4 + n) * B
                        last = nc.tensor.transpose(psT[0:r, at:at + B], acols[l][:, n, c0:c0 + r], T.ident[0:B, 0:B])
                last.then_inc(cols_ready, 1)


def wait_alone(eng, sem, value, passed):
    eng.wait_ge(sem, value)
    eng.sem_inc(passed, 1)


class Norm:

    def __init__(self, sb, sem):
        self.stats = sb("bn_stats", [P, TPB, 6], F32)
        self.mv = sb("mean_var", [P, TPB, 2], F32)
        self.veps = sb("var_eps", [P, TPB], F32)
        self.std = sb("std", [P, TPB], F32)
        self.rstd = sb("rstd", [P, TPB], F32)
        self.xn = sb("x_normed", [P, TPB, CX], F32)
        self.h = sb("h_mod", [P, KC, BLK], F32)
        self.steps = sem("norm_steps")
        self.passed = sem("waits_passed")
        self.var_ready = sem("var_ready")
        self.std_ready = sem("std_ready")
        self.xn_ready = sem("xn_ready")
        self.xt_ready = sem("xt_ready")
        self.h_ready = sem("h_ready")
        self.hi_ready = sem("hi_ready")
        self.parts_ready = sem("parts_ready")


def norm_variance(nc, dve, N, X, i):
    for t in range(TPB):
        last = nc.vector.bn_stats(N.stats[:, t, :], X[:, ds(i * TPB + t, 1), :].rearrange("p o c -> p (o c)"))
    last.then_inc(N.steps, 1)
    wait_alone(dve, N.steps, i * 3 + 1, N.passed)
    for t in range(TPB):
        last = nc.vector.bn_aggr(N.mv[:, t, :], N.stats[:, t, :])
    last.then_inc(N.steps, 1)
    dve.wait_ge(N.steps, i * 3 + 2)
    nc.vector.tensor_scalar(N.veps[:], N.mv[:, :, 1], EPS, None, ALU.add).then_inc(N.var_ready, 1)


def norm_tiles(nc, dve, N, X, i):
    dve.wait_ge(N.std_ready, i + 1)
    nc.vector.reciprocal(N.rstd[:], N.std[:]).then_inc(N.steps, 1)
    dve.wait_ge(N.steps, i * 3 + 3)
    dve.wait_ge(N.xt_ready, (i + 1) * KC)
    for t in range(TPB):
        x = X[:, ds(i * TPB + t, 1), :]
        again = x[:, :, FULL * P:C].broadcast_to([P, len(PARTS) - 1, REST])
        nc.vector.tensor_scalar(N.xn[:, t, 0:C], x.rearrange("p o c -> p (o c)"),
                                N.mv[:, t, 0:1], N.rstd[:, t:t + 1], ALU.subtract, ALU.mult)
        last = nc.vector.tensor_scalar(N.xn[:, t, C:CX].rearrange("p (o c) -> p o c", c=REST), again,
                                       N.mv[:, t, 0:1], N.rstd[:, t:t + 1], ALU.subtract, ALU.mult)
    last.then_inc(N.xn_ready, 1)


def norm_transposes(nc, pe, N, T, psT, i):
    pe.wait_ge(N.xn_ready, i + 1)
    for j, (c0, r) in enumerate(CHUNK):
        pe.wait_ge(N.h_ready, i * KC + j + 1)
        for t in range(TPB):
            last = nc.tensor.transpose(psT[j][0:r, t * P:(t + 1) * P], N.xn[:, t, c0:c0 + r], T.ident[:])
        last.then_inc(N.xt_ready, 1)


def norm_root(nc, act, N, i):
    act.wait_ge(N.var_ready, i + 1)
    nc.scalar.activation(N.std[:], N.veps[:], ACT.Sqrt).then_inc(N.std_ready, 1)


def norm_modulate(nc, act, N, mod, which, psT, b, hT, i):
    def high(j):
        act.wait_ge(N.h_ready, (i + 1) * KC + j + 1)
        nc.scalar.activation(hT(*part_places(j)[0]), N.h[0:CHUNK[j][1], j, :], ACT.Copy).then_inc(N.hi_ready, 1)

    for j, (_, r) in enumerate(CHUNK):
        act.wait_ge(N.xt_ready, (i + 1) * KC + j + 1)
        act.wait_ge(N.parts_ready, i * KC + j + 1)
        nc.scalar.activation(N.h[0:r, j, :], psT[j][0:r, :], ACT.Identity, scale=mod[0:r, which + 1, j, b],
                             bias=mod[0:r, which, j, b]).then_inc(N.h_ready, 1)
        if j:
            high(j - 1)
    high(KC - 1)


def part_places(j):
    return ((HI + j, slice(0, P)), (LO + j, slice(0, P))) if j < FULL else ((STK, slice(0, STACK)), (STK, H_LO))


def norm_low(nc, dve, N, hT, i):
    for j in range(KC):
        (hi, _), (lo, rows) = part_places(j)
        dve.wait_ge(N.hi_ready, i * KC + j + 1)
        nc.vector.tensor_tensor(hT(lo, rows), N.h[rows, j, :], hT(hi, rows).bitcast(F32), ALU.subtract
                                ).then_inc(N.parts_ready, 1)


def load_w_qkv(sp, T, W, sem):
    load_chunks(sp, lambda k: T.w_qkv[:, k, :], W.w_qkv, sem)


def split_weight(nc, eng, w, f32, whi, w_ready):
    for j, (_, r) in enumerate(CHUNK):
        hi, lo, part = (HI + j, LO + j, slice(0, P)) if j < FULL else (STK, STK, W_LO)
        nc.vector.tensor_copy(w[0:r, hi, :], f32[0:r, j, :]).then_inc(whi, 1)
        eng.wait_ge(whi, j + 1)
        nc.vector.tensor_tensor(w[part, lo, :], f32[part, j, :], w[part, hi, :].bitcast(F32), ALU.subtract
                                ).then_inc(w_ready, 1)


def over_blocks(eng, body):
    with eng.Fori(0, NBLK - 1) as i:
        body(i, True)
    body(NBLK - 1, False)


def entry(i):
    return slice(i // HALVES, i // HALVES + 1) if isinstance(i, int) else ds(i // HALVES, 1)


LOADS = 16 * ((HALVES + 1) * len(Q_TERMS) + 1)


def load_group(sp, T, g, Q, K, V, sem):
    for n, (q, k) in enumerate(zip(Q_TERMS, K_TERMS)):
        rows = slice(n * D, (n + 1) * D)
        for half in range(HALVES):
            sp.dma_start(Q[rows, half, :, :], T.qk_scr[g, 0, q, :, half * BLK:(half + 1) * BLK].rearrange(
                "(j d) n -> d j n", j=HG)).then_inc(sem, 16)
        sp.dma_start(K[rows, :, :], T.qk_scr[g, 1, k].rearrange("(j d) n -> d j n", j=HG)).then_inc(sem, 16)
    sp.dma_start(V[:], T.V[:, g]).then_inc(sem, 16)


def load_ones(sp, T, K, sem):
    sp.dma_start(K[ROWS:ROWS + 2, :, :], T.ones_rows[:]).then_inc(sem, 16)


QK_BANKS = 3


def qkv_stage(nc, T, l, W):
    with ExitStack() as ctx:
        sb, banks, sem = scopes(nc, ctx, f"qkv{l}")
        w = sb("wqkv_parts", [P, SLOT, 3 * C], F32R)
        bqk = sb("b_qk", [CHUNK_HEADS * D, QK_CHUNKS], F32)
        bv = sb("b_v", [P, C], F32)
        N = Norm(sb, sem)
        hT = sb("hT_parts", [P, SLOT, 2 * BLK], F32R)
        thirds = [sb(f"thirds{c}", [CHUNK_HEADS * D, 3, BLK], BF16) for c in range(QK_CHUNKS)]
        rest = [sb(f"rest{c}", [CHUNK_HEADS * D, BLK], F32) for c in range(QK_CHUNKS)]
        psT = banks("xT", KC)
        psQ = banks("qk", QK_BANKS)
        psV = banks("v", 2)

        b_in = sem("b_in")
        whi_ready = sem("whi_ready")
        w_ready = sem("w_ready")
        v_filled = sem("v_filled")
        qk_ready = sem("qk_ready")
        v_ready = sem("v_ready")
        v_out = sem("v_out")
        first_ready = sem("first_ready")
        rest_ready = sem("rest_ready")
        second_ready = sem("second_ready")
        thirds_ready = sem("thirds_ready")
        group_in = sem("first_group_in")
        stored = [sem(f"stored{c}") for c in range(QK_CHUNKS)]
        pieces = [len(chunk_pieces(c)) for c in range(QK_CHUNKS)]

        def hT_of(i):
            return lambda slot, rows: hT[rows, slot, ds(i % 2 * BLK, BLK)]

        block = ctx.enter_context(nc.Block())

        @block.sync
        def _(sp):
            for c in range(QK_CHUNKS):
                r = chunk_rows(c)
                c0 = c * CHUNK_HEADS * D
                sp.dma_start(bqk[0:r, c:c + 1], W.b_qkv[c0:c0 + r].rearrange("(p o) -> p o", o=1)).then_inc(b_in, 16)
            sp.dma_start(bv[:], row(W.b_qkv[2 * C:3 * C], P)).then_inc(b_in, 16)
            for b in range(B):
                with sp.Fori(0, HALVES) as half:
                    i = half + b * HALVES
                    for c in range(QK_CHUNKS):
                        sp.wait_ge(thirds_ready, (i + 1) * QK_CHUNKS + c + 1)
                        for r0, r, qk, hg, off in chunk_pieces(c):
                            dst = T.qk_scr[b * GPB + hg, qk, :, off:off + r, ds(half * BLK, BLK)]
                            sp.dma_start(dst.rearrange("t r n -> r t n"), thirds[c][r0:r0 + r, :, :]
                                         ).then_inc(stored[c], 16)
                if b == 0:
                    for c in range(QK_CHUNKS):
                        sp.wait_ge(stored[c], 16 * pieces[c] * (HALVES + 1))
                    sp.wait_ge(v_out, HALVES * TPB + 2)
                    sp.wait_ge(v_filled, 4)
                    load_ones(sp, T, T.KS0, group_in)
                    load_group(sp, T, 0, T.QS0, T.KS0, T.VG0, group_in)
            sp.wait_ge(group_in, LOADS + 16)
            for c in range(QK_CHUNKS):
                sp.wait_ge(stored[c], 16 * pieces[c] * (NBLK + 1))

        @block.gpsimd
        def _(pool):
            v = T.V[:].rearrange("p g k (j d) -> p (g k j) d", j=HG)
            nc.gpsimd.memset(v[:, :, D:D + 1], 1.0).then_inc(v_filled, 1)
            nc.gpsimd.memset(v[:, :, D + 1:32], 0.0).then_inc(v_filled, 1)
            nc.gpsimd.memset(T.ones_rows[:], 1.0).then_inc(v_filled, 1)
            nc.gpsimd.memset(T.wp[:], 0.0).then_inc(v_filled, 1)
            pool.wait_ge(v_filled, 4)
            pool.sem_inc(thirds_ready, QK_CHUNKS)
            with pool.Fori(0, NBLK) as i:
                for c in range(QK_CHUNKS):
                    r = chunk_rows(c)
                    pool.wait_ge(second_ready, i * QK_CHUNKS + c + 1)
                    nc.gpsimd.tensor_tensor(thirds[c][0:r, 2, :], rest[c][0:r, :], thirds[c][0:r, 1, :],
                                            ALU.subtract).then_inc(thirds_ready, 1)

        @block.scalar
        def _(act):
            act.sem_inc(N.h_ready, KC)
            for c in range(QK_CHUNKS):
                act.sem_inc(stored[c], 16 * pieces[c])
            norm_root(nc, act, N, 0)
            norm_modulate(nc, act, N, T.mod[l], 0, psT, entry(0), hT_of(0), 0)
            act.wait_ge(b_in, 16 * (QK_CHUNKS + 1))

            def body(i, more):
                def second(c):
                    r = chunk_rows(c)
                    act.wait_ge(rest_ready, i * QK_CHUNKS + c + 1)
                    nc.scalar.activation(thirds[c][0:r, 1, :], rest[c][0:r, :], ACT.Identity
                                         ).then_inc(second_ready, 1)

                if more:
                    norm_root(nc, act, N, i + 1)
                for c in range(QK_CHUNKS):
                    r = chunk_rows(c)
                    act.wait_ge(qk_ready, i * QK_CHUNKS + c + 1)
                    act.wait_ge(stored[c], (i + 1) * (16 * pieces[c]))
                    nc.scalar.activation(thirds[c][0:r, 0, :], psQ[c % QK_BANKS][0:r, :], ACT.Identity,
                                         bias=bqk[0:r, c:c + 1]).then_inc(first_ready, 1)
                    if c:
                        second(c - 1)
                second(QK_CHUNKS - 1)
                if more:
                    norm_modulate(nc, act, N, T.mod[l], 0, psT, entry(i + 1), hT_of(i + 1), i + 1)

            over_blocks(act, body)

        @block.vector
        def _(dve):
            dve.sem_inc(v_out, 2)
            dve.sem_inc(N.parts_ready, KC)
            norm_variance(nc, dve, N, T.X, 0)
            norm_tiles(nc, dve, N, T.X, 0)
            split_weight(nc, dve, w, T.w_qkv, whi_ready, w_ready)
            norm_low(nc, dve, N, hT_of(0), 0)
            dve.wait_ge(b_in, 16 * (QK_CHUNKS + 1))

            def body(i, more):
                if more:
                    norm_variance(nc, dve, N, T.X, i + 1)
                for c in range(QK_CHUNKS):
                    r = chunk_rows(c)
                    dve.wait_ge(first_ready, i * QK_CHUNKS + c + 1)
                    dve.wait_ge(thirds_ready, i * QK_CHUNKS + c + 1)
                    nc.vector.scalar_tensor_tensor(out=rest[c][0:r, :], in0=psQ[c % QK_BANKS][0:r, :],
                                                   scalar=bqk[0:r, c:c + 1], in1=thirds[c][0:r, 0, :],
                                                   op0=ALU.add, op1=ALU.subtract
                                                   ).then_inc(rest_ready, 1)
                    if more and c == 1:
                        norm_tiles(nc, dve, N, T.X, i + 1)
                b, half = (i // HALVES, i % HALVES)
                for t in range(TPB):
                    dve.wait_ge(v_ready, i * TPB + t + 1)
                    dst = T.V[:, ds(b * GPB, GPB), ds(half * TPB + t, 1), :].rearrange(
                        "p g o (j d) -> p (g o) j d", j=HG)[:, :, :, 0:D]
                    nc.vector.tensor_tensor(dst, psV[t % 2][:, 0:C].rearrange("p (g j d) -> p g j d", g=GPB, j=HG),
                                            bv[:].rearrange("p (g j d) -> p g j d", g=GPB, j=HG),
                                            ALU.add).then_inc(v_out, 1)
                    if more and t == 2:
                        norm_low(nc, dve, N, hT_of(i + 1), i + 1)

            over_blocks(dve, body)

        @block.tensor
        def _(pe):
            pe.sem_inc(N.xt_ready, KC)
            norm_transposes(nc, pe, N, T, psT, 0)
            pe.wait_ge(w_ready, KC)

            for i in range(NBLK):
                at = i % 2 * BLK
                for c in range(QK_CHUNKS):
                    r = chunk_rows(c)
                    c0 = c * CHUNK_HEADS * D
                    if c >= QK_BANKS:
                        pe.wait_ge(rest_ready, i * QK_CHUNKS + c - QK_BANKS + 1)
                    for n, (ws, hs, rows) in enumerate(PASSES):
                        if c == 0 and n % len(PARTS) == 0:
                            pe.wait_ge(N.parts_ready, (i + 1) * KC + n // len(PARTS) + 1)
                        last = nc.tensor.matmul(psQ[c % QK_BANKS][0:r, :], w[0:rows, ws, c0:c0 + r], hT[0:rows, hs, at:at + BLK],
                                                start=(n == 0), stop=(n == len(PASSES) - 1))
                    last.then_inc(qk_ready, 1)
                if i + 1 < NBLK:
                    norm_transposes(nc, pe, N, T, psT, i + 1)
                for t in range(TPB):
                    pe.wait_ge(v_out, i * TPB + t + 1)
                    for n, (ws, hs, rows) in enumerate(PASSES):
                        last = nc.tensor.matmul(psV[t % 2][:, 0:C], hT[0:rows, hs, at + t * P:at + (t + 1) * P],
                                                w[0:rows, ws, 2 * C:3 * C], start=(n == 0), stop=(n == len(PASSES) - 1))
                    last.then_inc(v_ready, 1)
                pe.wait_ge(rest_ready, i * QK_CHUNKS + QK_CHUNKS)


SLOTS = 3
assert HG * HALVES * KT % SLOTS == 1
STEPS = HALVES * KT
PORTION = HG * TPB * 2
PER_STEP = 4
AHEAD = 8
assert PORTION * HALVES == PER_STEP * STEPS and (PORTION + 1) % SLOTS == 0


def max_work(first, end, last=False):
    for k in range(first, end):
        n, m = divmod(k, PORTION)
        before = ("join", n > 1, n % HALVES, None), ("turn", n > 1, n % HALVES, None)
        if n >= 0 and m in (0, 2) and not (last and n > 1):
            yield before[m // 2]
        if not (last and n > 0):
            yield "row", n > 0, (n + 1) % HALVES, m


COPY_STEP, RECIP_STEP, SPREAD_STEP, DIVIDE_STEP = KT + 1, KT + 3, KT + 5, KT + 7
UNIT = 2


def attention_stage(nc, T, l, W):
    with ExitStack() as ctx:
        sb, banks, sem = scopes(nc, ctx, f"att{l}")
        QS = [T.QS0] + [sb(f"QS{s}", [P, HALVES, HG, BLK], BF16) for s in range(1, SLOTS)]
        KS = [T.KS0] + [sb(f"KS{s}", [P, HG, SEQ], BF16) for s in range(1, SLOTS)]
        VG = [T.VG0] + [sb(f"VG{s}", [P, KT, HG * 32], F32) for s in range(1, SLOTS)]
        PR = [sb(f"probs{s}", [P, HG, BLK], F32) for s in range(2)]
        mx = [sb(f"mx{half}", [P, HG * TPB, 2], F32) for half in range(HALVES)]
        negm = sb("neg_max", [P, HG * TPB], F32)
        mrow = sb("neg_max_rows", [HG * TPB, 2, P], BF16)
        OZ = [sb(f"OZ{s}", [P, BLK], F32) for s in range(HALVES)]
        sums = [sb(f"sums{s}", [P, HG * BLK // P], F32) for s in range(HALVES)]
        inv = [sb(f"inverse{s}", [P, HG * BLK // P], F32) for s in range(HALVES)]
        RR = [sb(f"inverse_rows{s}", [P, BLK], F32) for s in range(HALVES)]
        psS = banks("scores", SLOTS)
        psM = banks("for_max", SLOTS)
        psO = banks("out", HALVES)

        ones_in = sem("ones_in")
        loaded = [sem(f"loaded{s}") for s in range(SLOTS)]
        m_loaded = [sem(f"m_loaded{half}") for half in range(HALVES)]
        scores_ready = sem("scores_ready")
        exp_done = sem("exp_done")
        pv_done = sem("pv_done")
        row_ready = sem("row_ready")
        row_read = sem("row_read")
        negm_ready = sem("negm_ready")
        mT_ready = sem("mT_ready")
        mhi_ready = sem("mhi_ready")
        mrow_ready = sem("mrow_ready")
        oz_ready = sem("oz_ready")
        rows_zero = sem("rows_zero")
        sums_in = [sem(f"sums_in{s}") for s in range(HALVES)]
        inv_ready = [sem(f"inv_ready{s}") for s in range(HALVES)]
        inv_in = [sem(f"inv_in{s}") for s in range(HALVES)]
        z_ready = sem("z_ready")
        o_ready = sem("o_ready")
        wp_in = sem("wp_in")

        def over_groups(eng, body):
            body(0, 0, 0)
            with eng.Fori(0, (GROUPS - 2) // SLOTS) as it:
                for n in range(1, SLOTS + 1):
                    body(it * SLOTS + n, n % SLOTS, it + n // SLOTS)
            body(GROUPS - 1, (GROUPS - 1) % SLOTS, (GROUPS - 1) // SLOTS)

        def score_bank(s, st, j):
            return psS[(s + st * HG + j) % SLOTS]

        def max_bank(m):
            return psM[m % SLOTS]

        turned = max_bank(PORTION)[0:HG * TPB, 0:P]

        def is_first(g):
            return isinstance(g, int) and g == 0

        def is_last(g):
            return isinstance(g, int) and g == GROUPS - 1

        def next_of(s, use):
            return (s + 1) % SLOTS, use + (s + 1) // SLOTS

        block = ctx.enter_context(nc.Block())

        @block.sync
        def _(sp):
            def store_max(g, half):
                for e in range(2):
                    if e == 0:
                        sp.wait_ge(mhi_ready, g * 2 + half + 1)
                    else:
                        sp.wait_ge(mrow_ready, g * 2 + half + 2)
                    sp.dma_start(QS[g % SLOTS][ROWS + e:ROWS + e + 1, half, :, :], mrow[:, e, :]
                                 ).then_inc(m_loaded[half], 16)

            def turn_sums(g, half):
                rows = slice(D, P, 32)
                sp.wait_ge(oz_ready, g * 2 + half + 1)
                sp.dma_start(sums[half][:], OZ[half][rows, :]).then_inc(sums_in[half], 16)
                if g == 0:
                    sp.wait_ge(rows_zero, HALVES)
                sp.wait_ge(inv_ready[half], g + 1)
                sp.dma_start(RR[half][rows, :], inv[half][:]).then_inc(inv_in[half], 16)

            for g in range(1, SLOTS):
                load_ones(sp, T, KS[g], ones_in)
            for j in range(HG):
                for g in range(GPB):
                    h = g * HG + j
                    sp.dma_start(T.wp[32 * j:32 * j + D, g, :], W.w_proj[h * D:(h + 1) * D, :]).then_inc(wp_in, 16)
            sp.dma_start(T.wp[D:D + 1, 0, :], row(W.b_proj, 1)).then_inc(wp_in, 16)
            store_max(0, 0)
            for g in range(GROUPS):
                if g:
                    turn_sums(g - 1, 1)
                store_max(g, 1)
                turn_sums(g, 0)
                if g + 1 < GROUPS:
                    store_max(g + 1, 0)
            turn_sums(GROUPS - 1, 1)
            for half in range(HALVES):
                sp.wait_ge(inv_in[half], 16 * GROUPS)
            sp.wait_ge(wp_in, 16 * (H + 1))

        @block.gpsimd
        def _(pool):
            for half in range(HALVES):
                nc.gpsimd.memset(RR[half][:], 0.0).then_inc(rows_zero, 1)
            for g in range(1, GROUPS):
                if g >= SLOTS:
                    pool.wait_ge(pv_done, (g - SLOTS + 1) * STEPS + 2)
                s = g % SLOTS
                load_group(pool, T, g, QS[s], KS[s], VG[s], loaded[s])

        @block.scalar
        def _(act):
            act.sem_inc(exp_done, UNIT * SLOTS)

            def finish(g, half):
                act.wait_ge(pv_done, g * STEPS + (half + 1) * KT + 2)
                act.wait_ge(o_ready, g * 2 + half + 1)
                nc.scalar.activation(OZ[half][:], psO[half][:], ACT.Copy).then_inc(oz_ready, 1)

            def body(g, s, use):
                for st in range(STEPS):
                    act.wait_ge(pv_done, g * STEPS + st + 1)
                    for j in range(HG):
                        act.wait_ge(scores_ready, g * (HG * STEPS) + HG * st + j + 1)
                        nc.scalar.activation(PR[st % 2][:, j, :], score_bank(s, st, j)[:], ACT.Exp, scale=SCALE
                                             ).then_inc(exp_done, UNIT)
                    if st == COPY_STEP:
                        finish(g, 0)
                    if st == COPY_STEP - KT and not is_first(g):
                        finish(g - 1, 1)

            over_groups(act, body)
            finish(GROUPS - 1, 1)

        @block.vector
        def _(dve):
            dve.sem_inc(row_read, SLOTS)
            dve.sem_inc(mrow_ready, 1)
            dve.sem_inc(o_ready, 2)

            def reduce(u, half, m):
                dve.wait_ge(row_ready, u * PORTION + m + 1)
                nc.vector.tensor_reduce(mx[half][:, m // 2, m % 2:m % 2 + 1], max_bank(m)[:], AX_X, ALU.max
                                        ).then_inc(row_read, 1)

            def join(u, half):
                dve.wait_ge(row_read, (u + 1) * PORTION + SLOTS)
                nc.vector.tensor_reduce(negm[:], mx[half][:], AX_X, ALU.max, negate=True).then_inc(negm_ready, 1)

            def rows_out(g, half):
                u = g * HALVES + half
                dve.wait_ge(mT_ready, u + 1)
                if half:
                    dve.wait_ge(m_loaded[0], 32 * g + 32)
                elif not is_first(g):
                    dve.wait_ge(m_loaded[1], 32 * g)
                nc.vector.tensor_copy(mrow[:, 0, :], turned).then_inc(mhi_ready, 1)
                dve.wait_ge(mhi_ready, u + 1)
                nc.vector.tensor_tensor(mrow[:, 1, :], turned, mrow[:, 0, :], ALU.subtract).then_inc(mrow_ready, 1)

            def maxima(g, first, end):
                for what, following, half, m in max_work(first, end, is_last(g)):
                    of = g + 1 if following else g
                    if what == "row":
                        reduce(of * HALVES + half, half, m)
                    elif what == "join":
                        join(of * HALVES + half, half)
                    else:
                        rows_out(of, half)

            def recip(g, half):
                dve.wait_ge(sums_in[half], 16 * g + 16)
                nc.vector.reciprocal(inv[half][:], sums[half][:]).then_inc(inv_ready[half], 1)

            def divide(g, half):
                dve.wait_ge(z_ready, g * 2 + half + 1)
                dst = T.O[:, g] if isinstance(g, int) else T.O[:, ds(g, 1)].rearrange("p o n -> p (o n)")
                nc.vector.tensor_tensor(dst[:, half * BLK:(half + 1) * BLK], OZ[half][:], psO[half][:], ALU.mult
                                        ).then_inc(o_ready, 1)

            maxima(0, -PORTION, AHEAD)

            def body(g, s, use):
                for st in range(STEPS):
                    maxima(g, AHEAD + st * PER_STEP, AHEAD + (st + 1) * PER_STEP)
                    for at, what in ((RECIP_STEP, recip), (DIVIDE_STEP, divide)):
                        if st == at - KT and not is_first(g):
                            what(g - 1, 1)
                        if st == at:
                            what(g, 0)

            over_groups(dve, body)
            recip(GROUPS - 1, 1)
            divide(GROUPS - 1, 1)

        @block.tensor
        def _(pe):
            pe.sem_inc(pv_done, 2)

            def max_row(g, s, half, m):
                u = g * HALVES + half
                j, t, keys = m // (2 * TPB), m // 2 % TPB, m % 2
                if m == 2:
                    pe.wait_ge(mrow_ready, u + 1)
                else:
                    pe.wait_ge(row_read, u * PORTION + m + (2 if m < 2 else 1))
                nc.tensor.matmul(max_bank(m)[:], QS[s][0:ROWS, half, j, t * P:(t + 1) * P],
                                 KS[s][0:ROWS, j, keys * BLK:(keys + 1) * BLK], start=True, stop=True
                                 ).then_inc(row_ready, 1)

            def turn(u):
                pe.wait_ge(negm_ready, u + 1)
                nc.tensor.transpose(turned, negm[:], T.ident[:]).then_inc(mT_ready, 1)

            def maxima(work, g, s, ns):
                while work:
                    what, following, half, m = work.pop(0)
                    of, slot = (g + 1, ns) if following else (g, s)
                    if what == "turn":
                        turn(of * HALVES + half)
                        return
                    if what == "row":
                        max_row(of, slot, half, m)
                        return

            def scores(g, s, st, j):
                half, k = divmod(st, KT)
                pe.wait_ge(exp_done, g * (UNIT * HG * STEPS) + UNIT * (HG * st + j + 1))
                nc.tensor.matmul(score_bank(s, st, j)[:], KS[s][0:ROWS + 2, j, k * P:(k + 1) * P],
                                 QS[s][0:ROWS + 2, half, j, :], start=True, stop=True
                                 ).then_inc(scores_ready, 1)

            def weigh(g, s, st, heads=range(HG)):
                half, k = divmod(st, KT)
                if k == 0 and 0 in heads:
                    pe.wait_ge(o_ready, g * 2 + half + 1)
                pe.wait_ge(exp_done, g * (UNIT * HG * STEPS) + UNIT * (HG * st + heads[-1] + 1 + SLOTS))
                for j in heads:
                    last = nc.tensor.matmul(psO[half][32 * j:32 * j + 32, :], VG[s][:, k, 32 * j:32 * j + 32],
                                            PR[st % 2][:, j, :], start=(k == 0), stop=(k == KT - 1),
                                            tile_position=(0, 32 * j))
                if heads[-1] == HG - 1:
                    last.then_inc(pv_done, 1)

            def spread(g, half):
                pe.wait_ge(inv_in[half], 16 * g + 16)
                nc.tensor.matmul(psO[half][:], T.sel[:], RR[half][:], start=True, stop=True).then_inc(z_ready, 1)

            pe.wait_ge(ones_in, 16 * (SLOTS - 1))
            work = list(max_work(-PORTION, AHEAD))
            while work:
                maxima(work, 0, 0, 1)

            def body(g, s, use):
                ns, nuse = next_of(s, use)
                for st in range(STEPS):
                    if st % KT == 0:
                        pe.wait_ge(m_loaded[st // KT], 32 * g + 32)
                    if AHEAD + st * PER_STEP == PORTION and not is_last(g):
                        pe.wait_ge(loaded[ns], (nuse + (1 if ns else 0)) * LOADS)
                    work = list(max_work(AHEAD + st * PER_STEP, AHEAD + (st + 1) * PER_STEP, is_last(g)))
                    last = (g, s, st - 1) if st else None if is_first(g) else (g - 1, (s - 1) % SLOTS, STEPS - 1)
                    scores(g, s, st, 0)
                    scores(g, s, st, 1)
                    maxima(work, g, s, ns)
                    scores(g, s, st, 2)
                    maxima(work, g, s, ns)
                    if last:
                        weigh(*last, range(0, HG // 2))
                    maxima(work, g, s, ns)
                    scores(g, s, st, 3)
                    if last:
                        weigh(*last, range(HG // 2, HG))
                    while work:
                        maxima(work, g, s, ns)
                    if st == SPREAD_STEP - KT and not is_first(g):
                        spread(g - 1, 1)
                    if st == SPREAD_STEP:
                        spread(g, 0)

            over_groups(pe, body)
            weigh(GROUPS - 1, (GROUPS - 1) % SLOTS, STEPS - 1)
            spread(GROUPS - 1, 1)


class Staging:

    def __init__(self, sb, sem):
        self.w1, self.w2 = sb("w1_f32", [P, FF], F32), sb("w2_f32", [P, NF // KC, C], F32)
        self.w1_in, self.w2_in = sem("w1_in"), sem("w2_in")
        self.w1_split, self.w2_split = sem("w1_split"), sem("w2_split")
        self.hi_ready = sem("w_hi_ready")


def load_expert(sp, S, W, e, n):
    w2 = W.w2[e].rearrange("(f p) n -> p f n", p=P)
    for k in range(KC):
        if n * KC + k:
            sp.wait_ge(S.w1_split, n * KC + k + 1)
        if k < FULL:
            sp.dma_start(S.w1[:], W.w1[e, k * P:(k + 1) * P]).then_inc(S.w1_in, 16)
        else:
            for m in range(len(PARTS)):
                sp.dma_start(S.w1[m * REST:(m + 1) * REST], W.w1[e, FULL * P:C]).then_inc(S.w1_in, 16)
        if n * KC + k:
            sp.wait_ge(S.w2_split, n * KC + k + 1)
        sp.dma_start(S.w2[:], w2[:, 3 * k:3 * k + 3, :]).then_inc(S.w2_in, 16)


def load_biases(sp, W, e, b1, b2, sem):
    sp.dma_start(b1[:], W.b1[e].rearrange("(f p) -> p f", p=P), allow_slow_non_contiguous=True).then_inc(sem, 16)
    sp.dma_start(b2[:], row(W.b2[e], P)).then_inc(sem, 16)


def split_expert(nc, pool, S, w1, w2, n):
    for k, (_, r) in enumerate(CHUNK):
        hi, lo, part = (HI + k, LO + k, slice(0, P)) if k < FULL else (STK, STK, W_LO)
        pool.wait_ge(S.w1_in, 16 * (n * CHUNK_LOADS + (k + 1 if k < FULL else CHUNK_LOADS)))
        nc.gpsimd.tensor_copy(w1[0:r, hi, :], S.w1[0:r]).then_inc(S.hi_ready, 1)
        pool.wait_ge(S.hi_ready, n * 2 * KC + 2 * k + 1)
        nc.gpsimd.tensor_tensor(w1[part, lo, :], S.w1[part], w1[part, hi, :].bitcast(F32), ALU.subtract
                                ).then_inc(S.w1_split, 1)
        if k == FULL:
            pool.wait_ge(S.w1_split, (n + 1) * KC + 1)
        f = slice(3 * k, 3 * k + 3)
        pool.wait_ge(S.w2_in, 16 * (n * KC + k + 1))
        nc.gpsimd.tensor_copy(w2[:, 0, f, :], S.w2[:]).then_inc(S.hi_ready, 1)
        pool.wait_ge(S.hi_ready, n * 2 * KC + 2 * k + 2)
        nc.gpsimd.tensor_tensor(w2[:, 1, f, :], S.w2[:], w2[:, 0, f, :].bitcast(F32), ALU.subtract
                                ).then_inc(S.w2_split, 1)


def project_stage(nc, T, l, W, moe):
    with ExitStack() as ctx:
        sb, banks, sem = scopes(nc, ctx, f"proj{l}")
        upd = sb("update", [P, TPB, C], F32)
        N = Norm(sb, sem)
        S = Staging(sb, sem)
        psT = banks("xT", KC)
        psP = banks("proj", TPB)
        psL = banks("logits", 1)[0]
        psLT = psL[:, 0:TPB * E]

        proj_ready = sem("proj_ready")
        gated = sem("gated")
        added = sem("added")
        bias_in = sem("bias_in")
        wg_in = sem("wg_in")
        wg_zero = sem("wg_zero")
        wghi_ready = sem("wghi_ready")
        wg_ready = sem("wg_ready")
        lg_ready = sem("lg_ready")
        lg_copied = sem("lg_copied")
        lgT_ready = sem("lgT_ready")
        lgT_read = sem("lgT_read")
        chain = sem("route_steps")
        ex_ready = sem("ex_ready")
        if moe:
            wgs = sb("w_gate_f32", [P, KC, P], F32)
            wg = sb("w_gate_parts", [P, SLOT, P], F32R)
            lg = sb("logits_sb", [E, BLK], F32)
            LG = sb("logits_all", [P, TILES, E], F32)
            rank = sb("rank", [P, TILES, E], F32)
            cmp = sb("cmp", [P, TILES], F32)
            top = sb("top", [P, TILES], F32)
            ex = sb("ex", [P, TILES, E], F32)
            den = sb("den", [P, TILES], F32)

        def over_inner_blocks(eng, body):
            body(0, False, True)
            with eng.Fori(1, NBLK - 1) as i:
                body(i, True, True)
            body(NBLK - 1, True, False)

        block = ctx.enter_context(nc.Block())

        @block.sync
        def _(sp):
            if moe:
                sp.wait_ge(wg_zero, 1)
                load_chunks(sp, lambda k: wgs[:, k, 0:E], W.w_gate, wg_in)
            load_expert(sp, S, W, 0, 0)
            load_biases(sp, W, 0, T.b1[0], T.b2[0], bias_in)
            sp.wait_ge(bias_in, 32)

        @block.gpsimd
        def _(pool):
            if moe:
                nc.gpsimd.memset(wgs[:], 0.0).then_inc(wg_zero, 1)
            pool.sem_inc(S.w1_split, 1)
            pool.sem_inc(S.w2_split, 1)
            split_expert(nc, pool, S, T.w1[0], T.w2[0], 0)

        @block.scalar
        def _(act):
            act.sem_inc(N.h_ready, KC)
            norm_root(nc, act, N, 0)

            def copy_logits(i):
                act.wait_ge(lg_ready, i + 1)
                nc.scalar.activation(lg[:], psL[0:E, :], ACT.Copy).then_inc(lg_copied, 1)

            def body(i, before, more):
                if more:
                    norm_root(nc, act, N, i + 1)
                if moe and before:
                    copy_logits(i - 1)
                norm_modulate(nc, act, N, T.mod[l], 2, psT, entry(i),
                              lambda slot, rows: T.hT[rows, slot, ds(i * BLK, BLK)], i)

            over_inner_blocks(act, body)
            if moe:
                copy_logits(NBLK - 1)
                act.wait_ge(chain, 2)
                nc.scalar.activation(ex[:], ex[:], ACT.Exp).then_inc(ex_ready, 1)

        @block.vector
        def _(dve):
            dve.sem_inc(N.parts_ready, KC)

            def update(i):
                for t in range(TPB):
                    dve.wait_ge(proj_ready, i * TPB + t + 1)
                    nc.vector.tensor_tensor(upd[:, t, :], psP[t][:, 0:C],
                                            T.gate[l][:, 0, entry(i), :].rearrange("p o c -> p (o c)"), ALU.mult
                                            ).then_inc(gated, 1)
                dve.wait_ge(gated, i * TPB + TPB)
                x = T.X[:, ds(i * TPB, TPB), :]
                nc.vector.tensor_tensor(x, x, upd[:], ALU.add).then_inc(added, 1)
                wait_alone(dve, added, i + 1, N.passed)
                norm_variance(nc, dve, N, T.X, i)
                norm_tiles(nc, dve, N, T.X, i)

            def copy_logits(i):
                dve.wait_ge(lgT_ready, i + 1)
                nc.vector.tensor_copy(LG[:, ds(i * TPB, TPB), :], psLT.rearrange("p (t e) -> p t e", e=E)
                                      ).then_inc(lgT_read, 1)

            update(0)
            if moe:
                dve.wait_ge(wg_in, 16 * CHUNK_LOADS)
                split_weight(nc, dve, wg, wgs, wghi_ready, wg_ready)

            def body(i, before, more):
                if more:
                    update(i + 1)
                norm_low(nc, dve, N, lambda slot, rows: T.hT[rows, slot, ds(i * BLK, BLK)], i)
                if moe and before:
                    copy_logits(i - 1)

            over_inner_blocks(dve, body)
            if not moe:
                return
            copy_logits(NBLK - 1)
            dve.wait_ge(lgT_read, NBLK)
            n = 0

            def step(ins):
                nonlocal n
                n += 1
                ins.then_inc(chain, 1)
                dve.wait_ge(chain, n)

            step(nc.vector.tensor_reduce(top[:], LG[:], AX_X, ALU.max))
            step(nc.vector.tensor_tensor(ex[:], LG[:], top[:].rearrange("p (t o) -> p t o", o=1).broadcast_to([P, TILES, E]),
                                         ALU.subtract))
            step(nc.vector.memset(rank[:], 0.0))
            for a in range(E):
                for c in range(a + 1, E):
                    step(nc.vector.tensor_tensor(cmp[:], LG[:, :, a], LG[:, :, c], ALU.is_ge))
                    step(nc.vector.tensor_tensor(rank[:, :, c], rank[:, :, c], cmp[:], ALU.add))
                    step(nc.vector.scalar_tensor_tensor(out=rank[:, :, a], in0=rank[:, :, a], scalar=1.0, in1=cmp[:],
                                                        op0=ALU.add, op1=ALU.subtract))
            step(nc.vector.tensor_scalar(rank[:], rank[:], 2.0, None, ALU.is_lt))
            dve.wait_ge(ex_ready, 1)
            step(nc.vector.tensor_tensor(ex[:], ex[:], rank[:], ALU.mult))
            step(nc.vector.reduce_sum(den[:], ex[:], AX_X))
            step(nc.vector.reciprocal(den[:], den[:]))
            step(nc.vector.tensor_tensor(T.cw[:], ex[:], den[:].rearrange("p (t o) -> p t o", o=1).broadcast_to([P, TILES, E]),
                                         ALU.mult))

        @block.tensor
        def _(pe):
            pe.sem_inc(N.xt_ready, KC)

            def project(i):
                b, half = divmod(i, HALVES)
                for t in range(TPB):
                    if i:
                        pe.wait_ge(gated, (i - 1) * TPB + t + 1)
                    at = half * BLK + t * P
                    for g in range(GPB):
                        last = nc.tensor.matmul(psP[t][:, 0:C], T.O[:, b * GPB + g, at:at + P], T.wp[:, g, :],
                                                start=(g == 0), stop=(g == GPB - 1))
                    last.then_inc(proj_ready, 1)

            def logits(i):
                pe.wait_ge(N.parts_ready, (i + 2) * KC)
                if i == 0:
                    pe.wait_ge(wg_ready, KC)
                else:
                    pe.wait_ge(lgT_read, i)
                for n, (ws, hs, rows) in enumerate(PASSES):
                    last = nc.tensor.matmul(psL[:], wg[0:rows, ws, :], T.hT[0:rows, hs, i * BLK:(i + 1) * BLK],
                                            start=(n == 0), stop=(n == len(PASSES) - 1))
                last.then_inc(lg_ready, 1)

            def turn_logits(i):
                pe.wait_ge(lg_copied, i + 1)
                for t in range(TPB):
                    last = nc.tensor.transpose(psLT[:, t * E:(t + 1) * E], lg[:, t * P:(t + 1) * P], T.ident[0:E, 0:E])
                last.then_inc(lgT_ready, 1)

            project(0)
            for i in range(NBLK):
                if i + 1 < NBLK:
                    project(i + 1)
                if moe and i:
                    logits(i - 1)
                norm_transposes(nc, pe, N, T, psT, i)
                if moe and i:
                    turn_logits(i - 1)
            if moe:
                logits(NBLK - 1)
                turn_logits(NBLK - 1)


def mlp_stage(nc, T, l, W, experts, following=None, out=None):
    with ExitStack() as ctx:
        sb, banks, sem = scopes(nc, ctx, f"mlp{l}")
        SETS = min(2, experts)
        RING = 3
        LAG = 2
        w1, w2, b1, b2 = T.w1, T.w2, T.b1, T.b2
        taken = 0

        def in_O(name, shape, dt):
            nonlocal taken
            n = shape[1] * (shape[2] if len(shape) == 3 else 1)
            ap = T.O[:].rearrange("p g n -> p (g n)")[:, taken:taken + n]
            taken += n
            return ap if len(shape) == 2 else ap.rearrange("p (a b) -> p a b", a=shape[1])

        if experts > 1:
            S = Staging(in_O, sem)
            w1 = [w1[0], sb("w1_parts1", [P, SLOT, FF], F32R)]
            w2 = [w2[0], sb("w2_parts1", [P, 2, NF, C], F32R)]
            b1 = [b1[0], sb("b1_1", [P, NF], F32)]
            b2 = [b2[0], sb("b2_1", [P, C], F32)]
        g32 = [in_O(f"gelu{n}", [P, BLK], F32) for n in range(RING)]
        upd = in_O("update", [P, TPB, C], F32)
        gb2 = in_O("gated_b2", [P, C], F32)
        hp = [sb(f"hidden_parts{n}", [P, 2, BLK], F32R) for n in range(RING)]
        psH = banks("hidden", RING)
        psY = banks("y", TPB)

        passed = sem("waits_passed")
        bias_in = [sem(f"bias_in{s}") for s in range(SETS)]
        bias_used = sem("bias_used")
        h_ready = sem("h_ready")
        gelu_ready = sem("gelu_ready")
        hi_ready = sem("hi_ready")
        parts_ready = sem("parts_ready")
        used = sem("hidden_used")
        y_read = sem("y_read")
        steps = sem("update_steps")
        stored = sem("stored")
        next_in = sem("next_in")

        def over_experts(eng, body):
            if experts == 1:
                body(0, 0, 0)
            else:
                with eng.Fori(0, experts // SETS) as it:
                    for s in range(SETS):
                        body(it * SETS + s, s, it)

        block = ctx.enter_context(nc.Block())

        @block.sync
        def _(sp):
            if following is not None:
                load_w_qkv(sp, T, following, next_in)
                sp.wait_ge(next_in, 16 * CHUNK_LOADS)
            if experts > 1:
                sp.sem_inc(bias_in[0], 32)
            for e in range(1, experts):
                load_expert(sp, S, W, e, e - 1)
                if e >= SETS:
                    sp.wait_ge(bias_used, e - SETS + 1)
                load_biases(sp, W, e, b1[e % SETS], b2[e % SETS], bias_in[e % SETS])
            if out is not None:
                rows = out.rearrange("b (t p) c -> p (b t) c", p=P)
                for i in range(NBLK):
                    sp.wait_ge(steps, ((experts - 1) * NBLK + i) * 3 + 3)
                    sp.dma_start(rows[:, i * TPB:(i + 1) * TPB], T.X[:, i * TPB:(i + 1) * TPB]).then_inc(stored, 16)
                sp.wait_ge(stored, 16 * NBLK)

        @block.gpsimd
        def _(pool):
            if experts > 1:
                pool.sem_inc(S.w1_split, 1)
                pool.sem_inc(S.w2_split, 1)
            for e in range(1, experts):
                if e >= SETS:
                    pool.wait_ge(used, (e - SETS + 1) * NBLK * NF + RING)
                split_expert(nc, pool, S, w1[e % SETS], w2[e % SETS], e - 1)

        @block.scalar
        def _(act):
            def body(e, s, use):
                if experts > 1:
                    act.wait_ge(bias_in[s], (use + 1) * 32)
                with act.Fori(0, NBLK) as i:
                    at = (e * NBLK + i) * NF
                    for f in range(NF):
                        act.wait_ge(h_ready, at + f + 1)
                        act.wait_ge(parts_ready, at + f + 1)
                        nc.scalar.activation(g32[f % RING][:], psH[f % RING][:], ACT.Gelu_apprx_tanh,
                                             bias=b1[s][:, f:f + 1]).then_inc(gelu_ready, 1)

            over_experts(act, body)

        @block.vector
        def _(dve):
            dve.sem_inc(parts_ready, RING)
            dve.sem_inc(y_read, TPB)

            def body(e, s, use):
                if experts > 1:
                    wait_alone(dve, bias_in[s], (use + 1) * 32, passed)
                with dve.Fori(0, NBLK) as i:
                    n = e * NBLK + i
                    gate = T.gate[l][:, 1, entry(i), :].rearrange("p o c -> p (o c)")

                    def weight(t):
                        return 1.0 if experts == 1 else \
                            T.cw[:, ds(i * TPB + t, 1), ds(e, 1)].rearrange("p t e -> p (t e)")

                    for f in range(NF):
                        dve.wait_ge(gelu_ready, n * NF + f + 1)
                        dve.wait_ge(used, n * NF + f + 1)
                        nc.vector.tensor_copy(hp[f % RING][:, 0, :], g32[f % RING][:]).then_inc(hi_ready, 1)
                        dve.wait_ge(hi_ready, n * NF + f + 1)
                        nc.vector.tensor_tensor(hp[f % RING][:, 1, :], g32[f % RING][:],
                                                hp[f % RING][:, 0, :].bitcast(F32), ALU.subtract
                                                ).then_inc(parts_ready, 1)
                        if f == NF // 2:
                            nc.vector.tensor_tensor(gb2[:], gate, b2[s][:], ALU.mult).then_inc(steps, 1)
                            dve.wait_ge(steps, n * 3 + 1)
                            for t in range(TPB):
                                x = T.X[:, ds(i * TPB + t, 1), :].rearrange("p o c -> p (o c)")
                                last = nc.vector.scalar_tensor_tensor(out=x, in0=gb2[:], scalar=weight(t), in1=x,
                                                                      op0=ALU.mult, op1=ALU.add)
                            last.then_inc(steps, 1)
                    dve.wait_ge(used, n * NF + NF + RING)
                    for t in range(TPB):
                        nc.vector.scalar_tensor_tensor(out=upd[:, t, :], in0=psY[t][:, 0:C], scalar=weight(t), in1=gate,
                                                       op0=ALU.mult, op1=ALU.mult).then_inc(y_read, 1)
                    dve.wait_ge(y_read, n * TPB + 2 * TPB)
                    dve.wait_ge(steps, n * 3 + 2)
                    x = T.X[:, ds(i * TPB, TPB), :]
                    nc.vector.tensor_tensor(x, x, upd[:], ALU.add).then_inc(steps, 1)
                dve.sem_inc(bias_used, 1)

            over_experts(dve, body)

        @block.tensor
        def _(pe):
            pe.sem_inc(used, RING)

            def body(e, s, use):
                if experts > 1:
                    pe.wait_ge(S.w1_split, e * KC + 1)
                    wait_alone(pe, S.w2_split, e * KC + 1, passed)
                with pe.Fori(0, NBLK) as i:
                    blk = e * NBLK + i

                    def up(f):
                        pe.wait_ge(parts_ready, blk * NF + f + 1)
                        for n, (ws, hs, rows) in enumerate(PASSES):
                            last = nc.tensor.matmul(psH[f % RING][:], w1[s][0:rows, ws, f * P:(f + 1) * P],
                                                    T.hT[0:rows, hs, ds(i * BLK, BLK)],
                                                    start=(n == 0), stop=(n == len(PASSES) - 1))
                        last.then_inc(h_ready, 1)

                    def down(f):
                        pe.wait_ge(parts_ready, blk * NF + f + 1 + RING)
                        for t in range(TPB):
                            if f == 0:
                                pe.wait_ge(y_read, blk * TPB + t + 1)
                            for n, (wpart, hpart) in enumerate(PARTS):
                                last = nc.tensor.matmul(psY[t][:, 0:C], hp[f % RING][:, hpart, t * P:(t + 1) * P],
                                                        w2[s][:, wpart, f, :], start=(f == 0 and n == 0),
                                                        stop=(f == NF - 1 and n == 2))
                        last.then_inc(used, 1)

                    for f in range(NF):
                        up(f)
                        if f >= LAG:
                            down(f - LAG)
                    for f in range(NF - LAG, NF):
                        down(f)

            over_experts(pe, body)


class Shared:
    pass


class Layer:

    def __init__(self, A, prefix, w_ada, b_ada, w_qkv, w_proj, w1, b1, w2, b2):
        self.w_ada, self.b_ada = A[prefix + w_ada], A[prefix + b_ada]
        self.w_qkv, self.b_qkv = A[prefix + w_qkv], A[prefix + "b_qkv"]
        self.w_proj, self.b_proj = A[prefix + w_proj], A[prefix + "b_proj"]
        self.w1, self.b1, self.w2, self.b2 = (A[prefix + n] for n in (w1, b1, w2, b2))
        if len(self.w1.shape) == 2:
            self.w1 = self.w1.rearrange("(o c) n -> o c n", o=1)
            self.b1 = self.b1.rearrange("(o c) -> o c", o=1)
            self.w2 = self.w2.rearrange("(o c) n -> o c n", o=1)
            self.b2 = self.b2.rearrange("(o c) -> o c", o=1)


def program(nc, A, out):
    layers = [Layer(A, "L0_cond_", "W_ada", "b_ada", "W_qkv", "W_proj", "W_fc1", "b_fc1", "W_fc2", "b_fc2"),
              Layer(A, "L1_cond_", "w_adaln", "b_adaln", "w_qkv", "w_proj", "w1", "b1", "w2", "b2")]
    layers[1].w_gate = A["L1_cond_w_gate"]
    with ExitStack() as ctx:
        sb = lambda name, shape, dt: ctx.enter_context(nc.sbuf_tensor(name, shape, dt))
        T = Shared()
        T.X = sb("X", [P, TILES, C], F32)
        T.ident = sb("ident", [P, P], F32)
        T.mod = [sb(f"mod{l}", [P, 4, KC, B], F32) for l in range(2)]
        T.gate = [sb(f"gate{l}", [P, 2, B, C], F32) for l in range(2)]
        T.cw = sb("expert_weights", [P, TILES, E], F32)
        T.sel = sb("sel", [P, P], F32)
        T.qk_scr = nc.dram_tensor("qk_thirds", (GROUPS, 2, 3, HG * D, SEQ), BF16).ap()
        T.O = sb("heads_out", [P, GROUPS, SEQ], F32)
        T.w_qkv = T.O[:].rearrange("p g n -> p (g n)")[:, GROUPS * SEQ - KC * 3 * C:].rearrange("p (k n) -> p k n", k=KC)
        T.wp = sb("w_proj", [P, GPB, C], F32)
        modulation(nc, T, A["x"], A["cond_1152"], layers)
        for l, W in enumerate(layers):
            own = lambda scope, name, shape, dt: scope.enter_context(nc.sbuf_tensor(f"{name}{l}", shape, dt))
            with ExitStack() as scope:
                T.V = own(scope, "V", [P, GROUPS, KT, HG * 32], F32)
                T.ones_rows = own(scope, "ones_rows", [2, HG, SEQ], BF16)
                T.QS0 = own(scope, "QS0_", [P, HALVES, HG, BLK], BF16)
                T.KS0 = own(scope, "KS0_", [P, HG, SEQ], BF16)
                T.VG0 = own(scope, "VG0_", [P, KT, HG * 32], F32)
                qkv_stage(nc, T, l, W)
                attention_stage(nc, T, l, W)
            with ExitStack() as scope:
                T.hT = own(scope, "hT", [P, SLOT, TOKENS], F32R)
                T.w1 = [own(scope, "w1_parts", [P, SLOT, FF], F32R)]
                T.w2 = [own(scope, "w2_parts", [P, 2, NF, C], F32R)]
                T.b1 = [own(scope, "b1", [P, NF], F32)]
                T.b2 = [own(scope, "b2", [P, C], F32)]
                project_stage(nc, T, l, W, moe=(l == 1))
                if l == 0:
                    mlp_stage(nc, T, l, W, 1, following=layers[1])
                else:
                    mlp_stage(nc, T, l, W, E, out=out)


_INS = ['x', 'cond_1152', 'L0_cond_W_qkv', 'L0_cond_b_qkv', 'L0_cond_W_proj', 'L0_cond_b_proj', 'L0_cond_W_fc1',
        'L0_cond_b_fc1', 'L0_cond_W_fc2', 'L0_cond_b_fc2', 'L0_cond_W_ada', 'L0_cond_b_ada', 'L1_cond_w_adaln',
        'L1_cond_b_adaln', 'L1_cond_w_qkv', 'L1_cond_b_qkv', 'L1_cond_w_proj', 'L1_cond_b_proj', 'L1_cond_w_gate',
        'L1_cond_w1', 'L1_cond_b1', 'L1_cond_w2', 'L1_cond_b2']


def kernel(**inputs):
    import numpy as _np
    import concourse.bacc as _bacc
    from concourse import mybir as _mybir
    from concourse.bass_utils import run_bass_kernel_spmd as _run

    nc = _bacc.Bacc("TRN2", target_bir_lowering=False, num_devices=1)
    arrays, args = {}, {}
    for name in _INS:
        a = _np.ascontiguousarray(inputs[name])
        arrays[f"in_{name}_dram"] = a
        args[name] = nc.dram_tensor(f"in_{name}_dram", a.shape, _mybir.dt.from_np(a.dtype), kind="ExternalInput").ap()
    out = nc.dram_tensor("out_0_dram", (B, SEQ, C), F32, kind="ExternalOutput").ap()
    program(nc, args, out)
    r = _run(nc, [arrays], core_ids=[0])
    return r.results[0]["out_0_dram"]
```
